# Optimizing a Trainium2 kernel written in Bass

```python
import numpy as np
import jax
import jax.numpy as jnp

def _softmax(x, axis=-1):
    return jax.nn.softmax(x, axis=axis)

def _gelu(x):
    return jax.nn.gelu(x, approximate=True)

def _silu(x):
    return jax.nn.silu(x)

def _sigmoid(x):
    return jax.nn.sigmoid(x)

def _layernorm(x, axis=-1, eps=1e-05):
    m = jnp.mean(x, axis=axis, keepdims=True)
    v = jnp.var(x, axis=axis, keepdims=True)
    return (x - m) / jnp.sqrt(v + eps)

def _scatter_add(tgt, idx, src, axis=0):
    return tgt.at[idx].add(src)

def _segment_sum(src, seg, n):
    return jax.ops.segment_sum(src, seg, n)
kernel_name = 'mk_adj_preln_d4_adj_r2_9712cf'

def setup_inputs(seed: int=0):
    np.random.seed(seed)
    _w = jnp.asarray

    def _rec_inputs():
        import jax
        import jax.numpy as jnp
        _gk = jax.random.key(seed)
        x = -0.000929 + 1 * jax.random.normal(jax.random.fold_in(_gk, 1), (4096, 128), jnp.float32)
        _a = jax.random.bernoulli(jax.random.fold_in(_gk, 2), 0.00390625, (4096, 4096))
        _a = jnp.logical_or(_a, jnp.eye(4096, dtype=bool))
        _af = _a.astype(jnp.float32)
        _af = _af * jax.random.uniform(jax.random.fold_in(_gk, 3), (4096, 4096), jnp.float32, 0.05, 1)
        adj = _af
        return (x, adj)
    x, adj = _rec_inputs()

    def _L0_gnn_setup():
        import jax, jax.numpy as jnp
        import numpy as np
        N, IN_DIM, OUT_DIM = (4096, 128, 128)
        key = jax.random.key(seed)
        k1, k2, k3, k4 = jax.random.split(key, 4)
        X = jax.random.normal(k1, (N, IN_DIM), dtype=jnp.float32)
        A = jax.random.uniform(k2, (N, N), dtype=jnp.float32)
        bound = 1.0 / np.sqrt(IN_DIM)
        W = jax.random.uniform(k3, (OUT_DIM, IN_DIM), minval=-bound, maxval=bound, dtype=jnp.float32)
        b = jax.random.uniform(k4, (OUT_DIM,), minval=-bound, maxval=bound, dtype=jnp.float32)
        return {'X': X, 'A': A, 'W': W, 'b': b}
    _L0_gnn_all = _L0_gnn_setup()
    _L0_gnn_in = {k: v for k, v in _L0_gnn_all.items() if k in ('W', 'b')}
    del _L0_gnn_all

    def _L1_gnn_setup():
        import jax, jax.numpy as jnp
        import numpy as np
        N, DIM = (8192, 128)

        def _gru_cell(x, h, W_ih, W_hh, b_ih, b_hh):
            gi = x @ W_ih.T + b_ih
            gh = h @ W_hh.T + b_hh
            i_r, i_z, i_n = jnp.split(gi, 3, axis=-1)
            h_r, h_z, h_n = jnp.split(gh, 3, axis=-1)
            r = jax.nn.sigmoid(i_r + h_r)
            z = jax.nn.sigmoid(i_z + h_z)
            n = jnp.tanh(i_n + r * h_n)
            return (1.0 - z) * n + z * h
        key = jax.random.key(seed)
        ks = jax.random.split(key, 8)
        states = jax.random.normal(ks[0], (N, DIM), dtype=jnp.float32)
        adj = jax.random.uniform(ks[1], (N, N), dtype=jnp.float32)
        s = 1.0 / np.sqrt(DIM)
        W_msg = jax.random.uniform(ks[2], (DIM, DIM), minval=-s, maxval=s, dtype=jnp.float32)
        b_msg = jax.random.uniform(ks[3], (DIM,), minval=-s, maxval=s, dtype=jnp.float32)
        W_ih = jax.random.uniform(ks[4], (3 * DIM, DIM), minval=-s, maxval=s, dtype=jnp.float32)
        W_hh = jax.random.uniform(ks[5], (3 * DIM, DIM), minval=-s, maxval=s, dtype=jnp.float32)
        b_ih = jax.random.uniform(ks[6], (3 * DIM,), minval=-s, maxval=s, dtype=jnp.float32)
        b_hh = jax.random.uniform(ks[7], (3 * DIM,), minval=-s, maxval=s, dtype=jnp.float32)
        return {'states': states, 'adj': adj, 'W_msg': W_msg, 'b_msg': b_msg, 'W_ih': W_ih, 'W_hh': W_hh, 'b_ih': b_ih, 'b_hh': b_hh}
    _L1_gnn_all = _L1_gnn_setup()
    _L1_gnn_in = {k: v for k, v in _L1_gnn_all.items() if k in ('W_msg', 'b_msg', 'W_ih', 'W_hh', 'b_ih', 'b_hh')}
    del _L1_gnn_all

    def _L2_gnn_setup():
        import jax, jax.numpy as jnp
        import numpy as np
        N = 8192
        IN_DIM = 128
        OUT_DIM = 128

        def _message(X, A, W):
            deg = jnp.sum(A, axis=1, keepdims=True)
            A_norm = A / jnp.where(deg > 0, deg, 1.0)
            return A_norm @ X @ W
        key = jax.random.key(seed)
        k1, k2, k3, k4 = jax.random.split(key, 4)
        X = jax.random.normal(k1, (N, IN_DIM), dtype=jnp.float32)
        A = jax.random.uniform(k2, (N, N), dtype=jnp.float32)
        W_in = jax.random.normal(k3, (IN_DIM, OUT_DIM), dtype=jnp.float32) / np.sqrt(IN_DIM)
        W_out = jax.random.normal(k4, (IN_DIM, OUT_DIM), dtype=jnp.float32) / np.sqrt(IN_DIM)
        return {'X': X, 'A': A, 'W_in': W_in, 'W_out': W_out}
    _L2_gnn_all = _L2_gnn_setup()
    _L2_gnn_in = {k: v for k, v in _L2_gnn_all.items() if k in ('W_in', 'W_out')}
    del _L2_gnn_all

    def _L3_gnn_setup():
        import jax, jax.numpy as jnp
        import numpy as np
        N = 4096
        H = 128
        key = jax.random.key(seed)
        k_x, k_A, k_W = jax.random.split(key, 3)
        x = jax.random.normal(k_x, (N, H), dtype=jnp.float32)
        A = jax.random.uniform(k_A, (N, N), dtype=jnp.float32)
        alpha = jnp.array([0.5], dtype=jnp.float32)
        bound = 1.0 / np.sqrt(H)
        W = jax.random.uniform(k_W, (H, H), dtype=jnp.float32, minval=-bound, maxval=bound)
        b = jnp.zeros((H,), dtype=jnp.float32)
        t = jnp.zeros((1,), dtype=jnp.float32)
        return {'t': t, 'x': x, 'A': A, 'alpha': alpha, 'W': W, 'b': b}
    _L3_gnn_all = _L3_gnn_setup()
    _L3_gnn_in = {k: v for k, v in _L3_gnn_all.items() if k in ('t', 'alpha', 'W', 'b')}
    del _L3_gnn_all
    return {'x': x, 'adj': adj, 'L0_gnn_W': _L0_gnn_in['W'], 'L0_gnn_b': _L0_gnn_in['b'], 'L1_gnn_W_msg': _L1_gnn_in['W_msg'], 'L1_gnn_b_msg': _L1_gnn_in['b_msg'], 'L1_gnn_W_ih': _L1_gnn_in['W_ih'], 'L1_gnn_W_hh': _L1_gnn_in['W_hh'], 'L1_gnn_b_ih': _L1_gnn_in['b_ih'], 'L1_gnn_b_hh': _L1_gnn_in['b_hh'], 'L2_gnn_W_in': _L2_gnn_in['W_in'], 'L2_gnn_W_out': _L2_gnn_in['W_out'], 'L3_gnn_t': _L3_gnn_in['t'], 'L3_gnn_alpha': _L3_gnn_in['alpha'], 'L3_gnn_W': _L3_gnn_in['W'], 'L3_gnn_b': _L3_gnn_in['b']}

def reference(x, adj, L0_gnn_W, L0_gnn_b, L1_gnn_W_msg, L1_gnn_b_msg, L1_gnn_W_ih, L1_gnn_W_hh, L1_gnn_b_ih, L1_gnn_b_hh, L2_gnn_W_in, L2_gnn_W_out, L3_gnn_t, L3_gnn_alpha, L3_gnn_W, L3_gnn_b):
    import jax
    import jax.numpy as jnp

    def _L0_gnn_ref(X, A, W, b):
        import jax, jax.numpy as jnp
        import numpy as np
        N, IN_DIM, OUT_DIM = (4096, 128, 128)
        n = A.shape[0]
        A_hat = A + jnp.eye(n, dtype=A.dtype)
        d_inv_sqrt = A_hat.sum(axis=1) ** (-0.5)
        A_norm = d_inv_sqrt[:, None] * A_hat * d_inv_sqrt[None, :]
        H = A_norm @ X
        return H @ W.T + b

    def _L1_gnn_ref(states, adj, W_msg, b_msg, W_ih, W_hh, b_ih, b_hh):
        import jax, jax.numpy as jnp
        import numpy as np
        N, DIM = (8192, 128)

        def _gru_cell(x, h, W_ih, W_hh, b_ih, b_hh):
            gi = x @ W_ih.T + b_ih
            gh = h @ W_hh.T + b_hh
            i_r, i_z, i_n = jnp.split(gi, 3, axis=-1)
            h_r, h_z, h_n = jnp.split(gh, 3, axis=-1)
            r = jax.nn.sigmoid(i_r + h_r)
            z = jax.nn.sigmoid(i_z + h_z)
            n = jnp.tanh(i_n + r * h_n)
            return (1.0 - z) * n + z * h
        agg = adj @ states
        msg = jax.nn.relu(agg @ W_msg.T + b_msg)
        return _gru_cell(msg, states, W_ih, W_hh, b_ih, b_hh)

    def _L2_gnn_ref(X, A, W_in, W_out):
        import jax, jax.numpy as jnp
        import numpy as np
        N = 8192
        IN_DIM = 128
        OUT_DIM = 128

        def _message(X, A, W):
            deg = jnp.sum(A, axis=1, keepdims=True)
            A_norm = A / jnp.where(deg > 0, deg, 1.0)
            return A_norm @ X @ W
        X_in = _message(X, A, W_in)
        X_out = _message(X, A.T, W_out)
        return X_in + X_out

    def _L3_gnn_ref(t, x, A, alpha, W, b):
        import jax, jax.numpy as jnp
        import numpy as np
        N = 4096
        H = 128
        a = alpha[0]
        A_prime = a * A
        diag = jnp.diagonal(A_prime) + (1.0 - a)
        A_prime = A_prime.at[jnp.arange(N), jnp.arange(N)].set(diag)
        out_degree = A_prime.sum(axis=1)
        inv_deg = jnp.where(out_degree == 0.0, 0.0, 1.0 / out_degree)
        x = inv_deg[:, None] * A_prime @ x
        x = x @ W.T + b
        return jax.nn.relu(x)
    h = jnp.maximum(_layernorm(x, axis=-1), 0.0)
    x = x + _L0_gnn_ref(h, adj, L0_gnn_W, L0_gnn_b)
    h = jnp.maximum(_layernorm(x, axis=-1), 0.0)
    x = x + _L1_gnn_ref(h, adj, L1_gnn_W_msg, L1_gnn_b_msg, L1_gnn_W_ih, L1_gnn_W_hh, L1_gnn_b_ih, L1_gnn_b_hh)
    h = jnp.maximum(_layernorm(x, axis=-1), 0.0)
    x = x + _L2_gnn_ref(h, adj, L2_gnn_W_in, L2_gnn_W_out)
    h = jnp.maximum(_layernorm(x, axis=-1), 0.0)
    x = x + _L3_gnn_ref(L3_gnn_t, h, adj, L3_gnn_alpha, L3_gnn_W, L3_gnn_b)
    return x

_drawn_inputs = setup_inputs


def setup_inputs(seed=0):
    import zlib

    import numpy as np

    out = dict(_drawn_inputs(seed))
    spreads = {'L3_gnn_b': (0.0, 0.1)}
    factors = {'L1_gnn_b_msg': 8.0, 'L1_gnn_b_ih': 3.903, 'L1_gnn_b_hh': 5.776}
    for name, (base, spread) in spreads.items():
        noise = np.random.default_rng([zlib.crc32(name.encode()), seed]).standard_normal(out[name].shape)
        drawn = base * np.exp(spread * noise) if base else spread * noise
        out[name] = jnp.asarray(drawn.astype(out[name].dtype))
    for name, factor in factors.items():
        out[name] = (out[name] * factor).astype(out[name].dtype)
    return out
```

```python
import concourse.bass as bass
from concourse import mybir
from contextlib import ExitStack

N = 4096
F = 128
P = 128
GC = 1024
NG = N // GC
GB = GC // P
NB = N // P
JB = 2
NU = NB // JB
BANK = 512
CH = GC // BANK
CB = BANK // P
RING = 4
UPG = NB // NG // JB
EPS = 1e-5
START = 1

TURN_AT, PROJECT_AT = 0, 1
MSG_AT, GATES_AT, MIX_AT = (1, 7), (3, 9), (7, 12)
TAKE_AT, HIGH_AT = 4, 9
ACT_MSG_AT, ACT_GATES_AT, ACT_NEW_AT = (5, 11), (8, 14), (9, 15)
GATHER_AT, RESIDUAL_AT, APPLY_AT, LOW_AT = 2, 6, 8, 10
DVE_NEW_AT, DVE_MIX_AT, DVE_GRU_AT = (9, 15), (10, 16), (12, 16)

W0, WMSG, WIH, WHH, WIN, WOUT, W3 = 0, 1, 2, 5, 8, 9, 10
NPAR = 11
BR0, BR3 = 0, 1
BMSG, BIH, BHH = 0, 1, 4
NCOL = 7


def build_gnn(nc, x_in, a_rows, a_cols, params, rows, alpha, out):
    F32, F32R, BF16 = mybir.dt.float32, mybir.dt.float32r, mybir.dt.bfloat16
    ACT = mybir.ActivationFunctionType
    ALU = mybir.AluOpType
    AX = mybir.AxisListType

    ctx = ExitStack()
    with ctx:
        def sb(name, shape, dt=F32):
            return ctx.enter_context(nc.sbuf_tensor(name, shape, dt))

        def sem(name):
            return ctx.enter_context(nc.semaphore(name))

        raw = sb("raw", [P, RING, JB * GC])
        a_high = sb("a_high", [P, RING, JB * GC], F32R)
        a_low = sb("a_low", [P, RING, JB * GC], F32R)
        x = sb("x", [P, NB, F])
        h_high = [sb(f"h_high{i}", [P, NB, F], F32R) for i in range(2)]
        h_low = [sb(f"h_low{i}", [P, NB, F], F32R) for i in range(2)]
        par = sb("par", [P, NPAR * P + NCOL])
        cols = par[:, NPAR * P:]
        brow = sb("brow", [P, 2, F])
        alpha_col = sb("alpha_col", [P, 1])
        y = sb("y", [P, GC])
        hs = sb("hs", [P, GB, F])
        hsT = sb("hsT", [P, GC])
        work = sb("work", [P, 2 * GC])
        row_acc = work[:, :]
        tn = work[:, 0:GC]
        upd = work[:, GC:2 * GC]
        msgT, gate_r, gate_z, new_n = (work[:, i * BANK:(i + 1) * BANK] for i in range(4))
        ident = sb("ident", [P, P])
        ones = sb("ones", [P, 1])
        rsum = sb("rsum", [P, NB])
        csum = sb("csum", [P, NB])
        cpart = sb("cpart", [P, NG, NB])
        scale = [sb(f"scale{i}", [P, NB]) for i in range(4)]
        flag = sb("flag", [P, 2, NB])
        gbias = sb("gbias", [P, 2])
        one_m_a = sb("one_m_a", [P, 1])
        stats = sb("stats", [P, GB, 6])
        mv = sb("mv", [P, GB, 2])
        veps = sb("veps", [P, GB])
        rstd = sb("rstd", [P, GB])
        shift = sb("shift", [P, GB])
        carrier = sb("carrier", [P, 2])
        mhalf = sb("mhalf", [P, GB])
        dplus = sb("dplus", [P, GB])
        dgrp = sb("dgrp", [P, GB])

        acc = ctx.enter_context(nc.psum_tensor("acc", [P, 2, GC], F32))
        E = ctx.enter_context(nc.psum_tensor("E", [P, 4, BANK], F32))

        def bank(i):
            return E[:, i, :]

        def w(i, n=1):
            return par[:, i * P:(i + n) * P]

        params_in = sem("params_in")
        rows_in = sem("rows_in")
        x_loaded = sem("x_loaded")
        consts = sem("consts")
        landed = [sem(f"landed{i}") for i in range(RING)]
        act_unit = sem("act_unit")
        half_unit = sem("half_unit")
        dve_unit = sem("dve_unit")
        pe_unit = sem("pe_unit")
        acc_taken = sem("acc_taken")
        rows_folded = sem("rows_folded")
        rows_saved = sem("rows_saved")
        d_ready = sem("d_ready")
        d_saved = sem("d_saved")
        carrier_set = sem("carrier_set")
        small = sem("small")
        stats_done = sem("stats_done")
        moments = sem("moments")
        var_ready = sem("var_ready")
        rstd_ready = sem("rstd_ready")
        shift_ready = sem("shift_ready")
        normed = sem("normed")
        added = sem("added")
        norm_ready = sem("norm_ready")
        high_ready = sem("high_ready")
        h_ready = sem("h_ready")
        self_ready = sem("self_ready")
        self_turned = sem("self_turned")
        selfT_ready = sem("selfT_ready")
        projected = sem("projected")
        scaled = sem("scaled")
        biased = sem("biased")
        x_new = sem("x_new")
        msg_done = sem("msg_done")
        msg_ready = sem("msg_ready")
        gates_done = sem("gates_done")
        r_ready = sem("r_ready")
        z_ready = sem("z_ready")
        reset_done = sem("reset_done")
        new_sum = sem("new_sum")
        n_ready = sem("n_ready")
        mixing = sem("mixing")
        mixed = sem("mixed")
        mix_turned = sem("mix_turned")
        x_gru = sem("x_gru")
        stored = sem("stored")

        LAYER_OF = [0, 1, 2, 2, 3]
        LAST = 4
        PROJ0 = {0: 0, 2: NG, 3: 2 * NG, 4: 3 * NG}
        SELF0 = {0: 0, 1: NG, 4: 2 * NG}
        LN0 = {0: NG, 1: 2 * NG, 3: 3 * NG}
        WEIGHT = {0: W0, 2: WIN, 3: WOUT, 4: W3}
        SCALE = {0: 0, 2: 1, 3: 2, 4: 3}

        SWEEP_UNITS = NG * NU

        def per_group(eng, body):
            body(0, True)
            with eng.Fori(1, NG) as g:
                body(g, False)

        block = ctx.enter_context(nc.Block())

        @block.sync
        def _(sp):
            sp.dma_start(x[:, :, :], x_in.rearrange("(b p) f -> p b f", p=P)).then_inc(x_loaded, 16)

            def load(src, g, first_unit, u, free=True):
                if free:
                    sp.wait_ge(act_unit, first_unit + u - RING + 1)
                    sp.wait_ge(dve_unit, first_unit + u - RING + 1)
                sp.dma_start(raw[:, u % RING, :], src[g * NU + u]).then_inc(landed[u % RING], 16)

            def store(g):
                sp.wait_ge(x_new, PROJ0[LAST] + g + 1)
                sp.dma_start(out.rearrange("(b p) f -> p b f", p=P)[:, bass.ts(g, GB), :],
                             x[:, bass.ts(g, GB), :]).then_inc(stored, 16)

            for u in range(NU):
                load(a_rows, 0, 0, u, u >= RING)
                if u == RING:
                    sp.dma_start(par[:, :], params).then_inc(params_in, 16)
                    for r in range(2):
                        sp.dma_start(brow[:, r, :], rows[r:r + 1, :].partition_broadcast(P)).then_inc(rows_in, 16)
                    sp.dma_start(alpha_col[:, 0:1], alpha.partition_broadcast(P)).then_inc(rows_in, 16)
            with sp.Fori(1, NG) as g:
                for u in range(NU):
                    load(a_rows, g, g * NU, u)
            with sp.Fori(1, 4) as sweep:
                with sp.Fori(0, NG) as g:
                    for u in range(NU):
                        load(a_rows, g, (sweep * NG + g) * NU, u)
            with sp.Fori(0, NG) as g:
                for u in range(NU):
                    load(a_cols, g, (g + 4 * NG) * NU, u)
            for u in range(NU):
                load(a_rows, 0, 5 * NG * NU, u)
            with sp.Fori(1, NG) as g:
                for u in range(NU):
                    load(a_rows, g, (g + 5 * NG) * NU, u)
                store(g - 1)
            store(NG - 1)
            sp.wait_ge(stored, 16 * NG)

        @block.gpsimd
        def _(pool):
            nc.gpsimd.memset(ones[:, :], 1.0).then_inc(consts, 1)
            nc.gpsimd.memset(mhalf[:, :], -0.5).then_inc(consts, 1)
            nc.gpsimd.memset(ident[:, :], 0.0).then_inc(consts, 1)
            pool.wait_ge(consts, 3)
            nc.gpsimd.affine_select(out=ident[:, :], in_=ident[:, :], compare_op=ALU.not_equal, fill=1.0,
                                    base=0, pattern=[[-1, P]], channel_multiplier=1).then_inc(consts, 1)

            def reciprocal_std(k):
                pool.wait_ge(var_ready, k + 1)
                nc.gpsimd.tensor_tensor(rstd[:, :], veps[:, :], mhalf[:, :], ALU.pow).then_inc(rstd_ready, 1)

            with pool.Fori(0, NG) as g:
                pool.wait_ge(rows_saved, START + g + 1)
                nc.gpsimd.tensor_tensor(dgrp[:, :], dplus[:, :], mhalf[:, :], ALU.pow).then_inc(d_ready, 1)
                reciprocal_std(g)
            with pool.Fori(NG, 4 * NG) as k:
                reciprocal_std(k)

        @block.scalar
        def _(act):
            for counter in (acc_taken, selfT_ready, z_ready):
                act.sem_inc(counter, START)

            def high_part(k, g, layer):
                act.wait_ge(norm_ready, k + 1)
                nc.scalar.activation(h_high[layer % 2][:, bass.ts(g, GB), :],
                                     tn.rearrange("p (b f) -> p b f", f=F), ACT.Relu).then_inc(high_ready, 1)

            def sum_group(g, first):
                for u in range(NU):
                    if u == RING and not first:
                        high_part(g - 1, g - 1, 0)
                    act.wait_ge(landed[u % RING], 16 * (g * (NU // RING) + u // RING + 1))
                    for jb, (copy, counted) in enumerate(((y, half_unit), (hsT, act_unit))):
                        if not (first and u == 0):
                            act.wait_ge(counted, g * NU + u)
                        col = u * JB + jb
                        nc.scalar.activation(copy[:, :], raw[:, u % RING, bass.ts(jb, GC)], ACT.Copy,
                                             accum_out=cpart[:, g, col:col + 1]).then_inc(counted, 1)

            per_group(act, sum_group)
            high_part(NG - 1, NG - 1, 0)
            act.wait_ge(params_in, 16)
            act.wait_ge(rows_in, 48)

            def take_product(p, g):
                n = p * NG + g
                act.wait_ge(pe_unit, (n + 1) * NU)
                if p == 1:
                    act.wait_ge(projected, START + NG)
                    act.wait_ge(msg_done, START + CH * g)
                else:
                    if p == 2:
                        act.wait_ge(msg_done, START + CH * NG)
                    act.wait_ge(projected, START + PROJ0[p] + g)
                src = acc[:, g % 2, :]
                if p == LAST:
                    nc.scalar.activation(y[:, :], src, ACT.Copy, scale=alpha_col[:, 0:1])\
                        .then_inc(acc_taken, 1)
                else:
                    nc.scalar.copy(y[:, :], src).then_inc(acc_taken, 1)
                if p in SELF0:
                    act.wait_ge(self_turned, START + SELF0[p] + g + 1)
                    if p == 1:
                        act.wait_ge(mixed, START + CH * g)
                    src = E[:, 2:4, :].rearrange("p a b -> p (a b)")
                    if p == LAST:
                        nc.scalar.activation(hsT[:, :], src, ACT.Copy, scale=one_m_a[:, 0:1])\
                            .then_inc(selfT_ready, 1)
                    else:
                        nc.scalar.copy(hsT[:, :], src).then_inc(selfT_ready, 1)

            def message(q, g):
                act.wait_ge(msg_done, START + q + 1)
                act.wait_ge(gates_done, START + q)
                act.wait_ge(h_ready, START + 2 * NG + g)
                nc.scalar.activation(msgT, bank(1), ACT.Relu, bias=cols[:, BMSG:BMSG + 1]).then_inc(msg_ready, 1)

            def gates(q):
                act.wait_ge(gates_done, START + q + 1)
                nc.scalar.activation(gate_r, bank(2), ACT.Sigmoid, bias=gbias[:, 0:1]).then_inc(r_ready, 1)
                nc.scalar.activation(gate_z, bank(3), ACT.Sigmoid, bias=gbias[:, 1:2]).then_inc(z_ready, 1)

            def new_state(q):
                act.wait_ge(new_sum, START + q + 1)
                nc.scalar.activation(new_n, new_n, ACT.Tanh, bias=cols[:, BIH + 2:BIH + 3]).then_inc(n_ready, 1)

            def epilogue(p, g, u):
                if u == TAKE_AT:
                    take_product(p, g)
                if p == 1:
                    for c in range(CH):
                        q = CH * g + c
                        if u == ACT_MSG_AT[c]:
                            message(q, g)
                        if u == ACT_GATES_AT[c]:
                            gates(q)
                        if u == ACT_NEW_AT[c]:
                            new_state(q)
                if p in LN0 and u == (NU if p == 1 else HIGH_AT):
                    high_part(LN0[p] + g, g, LAYER_OF[p] + 1)

            def product(p):
                def body(g, first):
                    n = p * NG + g
                    for u in range(NU + 1):
                        if not first:
                            epilogue(p, g - 1, u)
                        elif p > 0:
                            epilogue(p - 1, NG - 1, u)
                        if u == NU:
                            break
                        act.wait_ge(landed[u % RING], 16 * ((n + NG) * (NU // RING) + u // RING + 1))
                        if not (p == 0 and first and u < RING):
                            act.wait_ge(pe_unit, n * NU + u - RING + 1)
                        nc.scalar.copy(a_high[:, u % RING, :], raw[:, u % RING, :]).then_inc(act_unit, 1)
                per_group(act, body)

            for p in range(LAST + 1):
                product(p)
            take_product(LAST, NG - 1)

        @block.vector
        def _(dve):
            for counter in (mixed, new_sum, x_gru, scaled, h_ready, rows_saved):
                dve.sem_inc(counter, START)

            done = [0]

            def step(ins):
                done[0] += 1
                ins.then_inc(small, 1)
                dve.wait_ge(small, done[0])

            def blocks(flat):
                return flat.rearrange("p (b f) -> p b f", f=F)

            def per_node(col):
                return col.unsqueeze(2).to_broadcast([P, GB, F])

            def carry_wait():
                nc.vector.tensor_copy(carrier[:, 1:2], carrier[:, 0:1])

            def ln_stats(k, g):
                carry_wait()
                for b in range(GB):
                    last = nc.vector.bn_stats(stats[:, b, :], x[:, g * GB + b, :])
                last.then_inc(stats_done, 1)
                dve.wait_ge(stats_done, k + 1)
                carry_wait()
                for b in range(GB):
                    last = nc.vector.bn_aggr(mv[:, b, :], stats[:, b, :])
                last.then_inc(moments, 1)
                dve.wait_ge(moments, k + 1)
                nc.vector.tensor_scalar(veps[:, :], mv[:, :, 1], EPS, None, ALU.add).then_inc(var_ready, 1)

            def ln_apply(k, g):
                dve.wait_ge(rstd_ready, k + 1)
                nc.vector.scalar_tensor_tensor(out=shift[:, :], in0=mv[:, :, 0], scalar=-1.0, in1=rstd[:, :],
                                               op0=ALU.mult, op1=ALU.mult).then_inc(shift_ready, 1)
                dve.wait_ge(shift_ready, k + 1)
                for b in range(GB):
                    last = nc.vector.tensor_scalar(tn[:, bass.ts(b, F)], x[:, g * GB + b, :], rstd[:, b:b + 1],
                                                   shift[:, b:b + 1], ALU.mult, ALU.add)
                return last

            def low_part(k, g, layer):
                dve.wait_ge(high_ready, k + 1)
                nc.vector.scalar_tensor_tensor(
                    out=h_low[layer % 2][:, bass.ts(g, GB), :], in0=blocks(tn), scalar=0.0,
                    in1=h_high[layer % 2][:, bass.ts(g, GB), :].bitcast(F32),
                    op0=ALU.max, op1=ALU.subtract).then_inc(h_ready, 1)

            nc.vector.memset(carrier[:, :], 0.0).then_inc(carrier_set, 1)
            dve.wait_ge(carrier_set, 1)

            dve.wait_ge(x_loaded, 16)

            def sum_group(g):
                for u in range(1, NU):
                    if u == 1:
                        dve.wait_ge(h_ready, START + g)
                        dve.wait_ge(landed[0], 16 * (g * (NU // RING) + 1))
                    dve.wait_ge(landed[u % RING], 16 * (g * (NU // RING) + u // RING + 1))
                    if u == 1:
                        nc.vector.tensor_tensor(row_acc, raw[:, 0, :], raw[:, 1, :], ALU.add).then_inc(dve_unit, 2)
                    else:
                        dve.wait_ge(dve_unit, g * NU + u)
                        nc.vector.tensor_tensor(row_acc, row_acc, raw[:, u % RING, :], ALU.add)\
                            .then_inc(dve_unit, 1)
                ln_stats(g, g)
                dve.wait_ge(rows_folded, g + 1)
                nc.vector.tensor_copy(rsum[:, bass.ts(g, GB)], bank(3)[:, 0:GB])
                nc.vector.tensor_scalar(dplus[:, :], bank(3)[:, 0:GB], 1.0, None, ALU.add).then_inc(rows_saved, 1)
                ln_apply(g, g).then_inc(normed, 1)
                dve.wait_ge(d_ready, g + 1)
                dve.wait_ge(normed, g + 1)
                nc.vector.tensor_copy(scale[0][:, bass.ts(g, GB)], dgrp[:, :])
                for b in range(GB):
                    last = nc.vector.tensor_scalar(tn[:, bass.ts(b, F)], tn[:, bass.ts(b, F)], 0.0, dgrp[:, b:b + 1],
                                                   ALU.max, ALU.mult)
                last.then_inc(norm_ready, 1)
                dve.wait_ge(norm_ready, g + 1)
                dve.wait_ge(rows_in, 48)
                xg = x[:, bass.ts(g, GB), :]
                nc.vector.tensor_tensor(xg, xg, brow[:, BR0, :].unsqueeze(1).to_broadcast([P, GB, F]), ALU.add)\
                    .then_inc(added, 1)
                low_part(g, g, 0)

            with dve.Fori(0, NG) as g:
                sum_group(g)

            def degrees():
                dve.wait_ge(act_unit, SWEEP_UNITS)
                dve.wait_ge(params_in, 16)
                a = alpha_col[:, 0:1]
                step(nc.vector.tensor_tensor(gbias[:, :], cols[:, BIH:BIH + 2], cols[:, BHH:BHH + 2], ALU.add))
                step(nc.vector.tensor_scalar(one_m_a[:, :], a, -1.0, 1.0, ALU.mult, ALU.add))
                step(nc.vector.tensor_reduce(csum[:, :], cpart[:, :, :].rearrange("p g b -> p b g"), AX.X, ALU.add))
                for deg, sc in ((rsum, scale[1]), (csum, scale[2])):
                    step(nc.vector.tensor_scalar(flag[:, 0, :], deg[:, :], 0.0, None, ALU.is_gt))
                    step(nc.vector.tensor_scalar(flag[:, 1, :], flag[:, 0, :], -1.0, 1.0, ALU.mult, ALU.add))
                    step(nc.vector.tensor_tensor(flag[:, 0, :], flag[:, 0, :], deg[:, :], ALU.mult))
                    step(nc.vector.tensor_tensor(flag[:, 0, :], flag[:, 0, :], flag[:, 1, :], ALU.add))
                    step(nc.vector.reciprocal(sc[:, :], flag[:, 0, :]))
                step(nc.vector.tensor_scalar(scale[3][:, :], rsum[:, :], a, one_m_a[:, 0:1], ALU.mult, ALU.add))
                step(nc.vector.tensor_scalar(flag[:, 1, :], scale[3][:, :], 0.0, None, ALU.is_equal))
                step(nc.vector.tensor_tensor(flag[:, 0, :], scale[3][:, :], flag[:, 1, :], ALU.add))
                step(nc.vector.reciprocal(scale[3][:, :], flag[:, 0, :]))
                step(nc.vector.tensor_scalar(flag[:, 1, :], flag[:, 1, :], -1.0, 1.0, ALU.mult, ALU.add))
                step(nc.vector.tensor_tensor(scale[3][:, :], scale[3][:, :], flag[:, 1, :], ALU.mult))

            def gather_self(p, g):
                layer = LAYER_OF[p]
                dve.wait_ge(self_turned, START + SELF0[p] + g)
                nc.vector.tensor_tensor(hs[:, :, :], h_high[layer % 2][:, bass.ts(g, GB), :].bitcast(F32),
                                        h_low[layer % 2][:, bass.ts(g, GB), :].bitcast(F32), ALU.add)\
                    .then_inc(self_ready, 1)

            def residual(p, g):
                v = PROJ0[p] + g
                xg = x[:, bass.ts(g, GB), :]
                dve.wait_ge(projected, START + v + 1)
                nc.vector.tensor_tensor(blocks(upd), blocks(E[:, 0:2, :].rearrange("p a b -> p (a b)")),
                                        per_node(scale[SCALE[p]][:, bass.ts(g, GB)]), ALU.mult).then_inc(scaled, 1)
                dve.wait_ge(scaled, START + v + 1)
                if p == LAST:
                    nc.vector.tensor_tensor(blocks(upd), blocks(upd), brow[:, BR3, :].unsqueeze(1).to_broadcast([P, GB, F]),
                                            ALU.add).then_inc(biased, 1)
                    dve.wait_ge(biased, g + 1)
                    nc.vector.scalar_tensor_tensor(out=xg, in0=blocks(upd), scalar=0.0, in1=xg,
                                                   op0=ALU.max, op1=ALU.add).then_inc(x_new, 1)
                else:
                    nc.vector.tensor_tensor(xg, xg, blocks(upd), ALU.add).then_inc(x_new, 1)
                    dve.wait_ge(x_new, v + 1)

            def new_state(q):
                dve.wait_ge(r_ready, q + 1)
                nc.vector.scalar_tensor_tensor(out=new_n, in0=bank(0), scalar=cols[:, BHH + 2:BHH + 3], in1=gate_r,
                                               op0=ALU.add, op1=ALU.mult).then_inc(reset_done, 1)
                dve.wait_ge(reset_done, q + 1)
                nc.vector.tensor_tensor(new_n, new_n, bank(1), ALU.add).then_inc(new_sum, 1)

            def mix(q, c):
                dve.wait_ge(n_ready, q + 1)
                nc.vector.tensor_tensor(gate_r, hsT[:, bass.ts(c, BANK)], new_n, ALU.subtract).then_inc(mixing, 1)
                dve.wait_ge(mixing, 2 * q + 1)
                nc.vector.tensor_tensor(gate_r, gate_r, gate_z, ALU.mult).then_inc(mixing, 1)
                dve.wait_ge(mixing, 2 * q + 2)
                nc.vector.tensor_tensor(gate_r, gate_r, new_n, ALU.add).then_inc(mixed, 1)

            def gru_residual(q, g, c):
                xc = x[:, bass.ds(g * GB + c * CB, CB), :]
                dve.wait_ge(mix_turned, q + 1)
                nc.vector.tensor_tensor(xc, xc, blocks(bank(2)), ALU.add).then_inc(x_gru, 1)

            def epilogue(p, g, u):
                if p in SELF0 and u == GATHER_AT:
                    gather_self(p, g)
                if p in PROJ0 and u == RESIDUAL_AT:
                    residual(p, g)
                if p == 1:
                    for c in range(CH):
                        q = CH * g + c
                        if u == DVE_NEW_AT[c]:
                            new_state(q)
                        if u == DVE_MIX_AT[c]:
                            mix(q, c)
                        if u == DVE_GRU_AT[c]:
                            gru_residual(q, g, c)
                    if u == NU:
                        dve.wait_ge(x_gru, START + CH * (g + 1))
                if p in LN0:
                    k, layer = LN0[p] + g, LAYER_OF[p] + 1
                    if u == (NU if p == 1 else RESIDUAL_AT):
                        ln_stats(k, g)
                    if u == (NU if p == 1 else APPLY_AT):
                        ln_apply(k, g).then_inc(norm_ready, 1)
                    if u == (NU if p == 1 else LOW_AT):
                        low_part(k, g, layer)

            def product(p):
                def body(g, first):
                    n = p * NG + g
                    for u in range(NU + 1):
                        if not first:
                            epilogue(p, g - 1, u)
                        elif p > 0:
                            epilogue(p - 1, NG - 1, u)
                        elif u == RING:
                            degrees()
                        if u == NU:
                            break
                        dve.wait_ge(act_unit, SWEEP_UNITS + n * NU + u + 1)
                        if not (p == 0 and first and u < RING):
                            dve.wait_ge(pe_unit, n * NU + u - RING + 1)
                        nc.vector.tensor_tensor(a_low[:, u % RING, :], raw[:, u % RING, :],
                                                a_high[:, u % RING, :].bitcast(F32), ALU.subtract)\
                            .then_inc(dve_unit, 1)
                per_group(dve, body)

            for p in range(LAST + 1):
                product(p)
            gather_self(LAST, NG - 1)
            residual(LAST, NG - 1)

        @block.tensor
        def _(pe):
            for counter in (projected, self_turned, msg_done, gates_done):
                pe.sem_inc(counter, START)
            pe.wait_ge(consts, 4)

            with pe.Fori(0, NG) as g:
                pe.wait_ge(dve_unit, (g + 1) * NU)
                pe.wait_ge(rows_saved, START + g)
                for b in range(GB):
                    for jb in range(JB):
                        last = nc.tensor.matmul(bank(3)[:, b:b + 1], row_acc[:, bass.ds(jb * GC + b * P, P)],
                                                ones[:, 0:1], start=jb == 0, stop=jb == JB - 1)
                last.then_inc(rows_folded, 1)
            pe.wait_ge(params_in, 16)

            def turn_self(p, g):
                s = SELF0[p] + g
                pe.wait_ge(self_ready, s + 1)
                if p == 0:
                    pe.wait_ge(rows_saved, START + NG)
                else:
                    pe.wait_ge(z_ready, START + CH * (g if p == 1 else NG))
                    pe.wait_ge(x_gru, START + CH * (g if p == 1 else NG))
                pe.wait_ge(selfT_ready, START + s)
                for b in range(GB):
                    last = nc.tensor.transpose(bank(2 + b // CB)[:, bass.ts(b % CB, P)], hs[:, b, :], ident[:, :])
                last.then_inc(self_turned, 1)

            def project(p, g):
                v = PROJ0[p] + g
                pe.wait_ge(acc_taken, START + p * NG + g + 1)
                if p == 2:
                    pe.wait_ge(new_sum, START + CH * NG)
                pe.wait_ge(scaled, START + v)
                if p in SELF0:
                    pe.wait_ge(selfT_ready, START + SELF0[p] + g + 1)
                for b in range(GB):
                    o = bank(b // CB)[:, bass.ts(b % CB, P)]
                    last = nc.tensor.matmul(o, y[:, bass.ts(b, P)], w(WEIGHT[p]), start=True, stop=p not in SELF0)
                    if p in SELF0:
                        last = nc.tensor.matmul(o, hsT[:, bass.ts(b, P)], w(WEIGHT[p]), start=False, stop=True)
                last.then_inc(projected, 1)

            def message(q, g, c):
                pe.wait_ge(acc_taken, START + NG + g + 1)
                pe.wait_ge(scaled, START + NG)
                pe.wait_ge(new_sum, START + q)
                nc.tensor.matmul(bank(1), w(WMSG), y[:, bass.ts(c, BANK)], start=True, stop=True)\
                    .then_inc(msg_done, 1)

            def gates(q, g, c):
                m, h = msgT, hsT[:, bass.ts(c, BANK)]
                pe.wait_ge(selfT_ready, START + SELF0[1] + g + 1)
                pe.wait_ge(msg_ready, q + 1)
                pe.wait_ge(x_gru, START + q)
                for i in range(2):
                    nc.tensor.matmul(bank(2 + i), w(WIH + i), m, start=True, stop=False)
                    nc.tensor.matmul(bank(2 + i), w(WHH + i), h, start=False, stop=True)
                nc.tensor.matmul(bank(0), w(WHH + 2), h, start=True, stop=True)
                nc.tensor.matmul(bank(1), w(WIH + 2), m, start=True, stop=True).then_inc(gates_done, 1)

            def turn_mix(q):
                pe.wait_ge(mixed, START + q + 1)
                for b in range(CB):
                    last = nc.tensor.transpose(bank(2)[:, bass.ts(b, P)], gate_r[:, bass.ts(b, P)], ident[:, :])
                last.then_inc(mix_turned, 1)

            def epilogue(p, g, u):
                if p in SELF0 and u == TURN_AT:
                    turn_self(p, g)
                if p in PROJ0 and u == PROJECT_AT:
                    project(p, g)
                if p == 1:
                    for c in range(CH):
                        q = CH * g + c
                        if u == MSG_AT[c]:
                            message(q, g, c)
                        if u == GATES_AT[c]:
                            gates(q, g, c)
                        if u == MIX_AT[c]:
                            turn_mix(q)

            def product(p):
                layer = LAYER_OF[p]
                high, low = h_high[layer % 2], h_low[layer % 2]

                def body(g, first):
                    n = p * NG + g
                    out_banks = [acc[:, g % 2, bass.ts(c, BANK)] for c in range(CH)]
                    for u in range(NU):
                        if not first:
                            epilogue(p, g - 1, u)
                        elif p > 0:
                            epilogue(p - 1, NG - 1, u)
                        if first and u % UPG == 0 and p != 3:
                            pe.wait_ge(h_ready, START + layer * NG + u // UPG + 1)
                        if u == 0 and not (p == 0 and first):
                            pe.wait_ge(acc_taken, START + n - 1)
                        slot = u % RING
                        pe.wait_ge(act_unit, SWEEP_UNITS + n * NU + u + 1)
                        for jb in range(JB):
                            for hpart in (high, low):
                                for c in range(CH):
                                    nc.tensor.matmul(out_banks[c], hpart[:, u * JB + jb, :],
                                                     a_high[:, slot, bass.ds(jb * GC + c * BANK, BANK)],
                                                     start=u == 0 and jb == 0 and hpart is high, stop=False)
                        pe.wait_ge(dve_unit, SWEEP_UNITS + n * NU + u + 1)
                        for jb in range(JB):
                            for c in range(CH):
                                last = nc.tensor.matmul(out_banks[c], high[:, u * JB + jb, :],
                                                        a_low[:, slot, bass.ds(jb * GC + c * BANK, BANK)],
                                                        start=False, stop=u == NU - 1 and jb == JB - 1)
                        last.then_inc(pe_unit, 1)
                per_group(pe, body)

            for p in range(LAST + 1):
                product(p)
            turn_self(LAST, NG - 1)
            project(LAST, NG - 1)


def kernel(**inputs):
    import numpy as np
    import concourse.bacc as bacc
    from concourse.bass_utils import run_bass_kernel_spmd

    def tiles(a):
        return np.ascontiguousarray(
            a.reshape(NU, JB, P, NG, GC).transpose(3, 0, 2, 1, 4).reshape(NG * NU, P, JB * GC))

    a = {k: np.asarray(v) for k, v in inputs.items()}
    params = np.concatenate([
        a["L0_gnn_W"].T, a["L1_gnn_W_msg"].T, a["L1_gnn_W_ih"].T, a["L1_gnn_W_hh"].T, a["L2_gnn_W_in"],
        a["L2_gnn_W_out"], a["L3_gnn_W"].T, a["L1_gnn_b_msg"][:, None], a["L1_gnn_b_ih"].reshape(3, F).T,
        a["L1_gnn_b_hh"].reshape(3, F).T], axis=1)
    arrays = {
        "x_in": np.ascontiguousarray(a["x"]), "a_rows": tiles(a["adj"].T), "a_cols": tiles(a["adj"]),
        "params": np.ascontiguousarray(params), "rows": np.stack([a["L0_gnn_b"], a["L3_gnn_b"]]),
        "alpha": a["L3_gnn_alpha"].reshape(1, 1),
    }
    nc = bacc.Bacc("TRN2", target_bir_lowering=False, num_devices=1)
    f32 = mybir.dt.float32
    aps = {k: nc.dram_tensor(k, v.shape, f32, kind="ExternalInput").ap() for k, v in arrays.items()}
    out = nc.dram_tensor("out", (N, F), f32, kind="ExternalOutput").ap()
    build_gnn(nc, out=out, **aps)
    r = run_bass_kernel_spmd(nc, [arrays], core_ids=[0])
    return r.results[0]["out"]
```

```python
import concourse.bass as bass
from concourse import mybir
from contextlib import ExitStack

N = 4096
F = 128
P = 128
GC = 1024
NG = N // GC
GB = GC // P
NB = N // P
JB = 2
VU = GC // (JB * P)
NU = NB // JB
BANK = 512
CH = GC // BANK
CB = BANK // P
RAW = 4
SPLIT = 3
EPS = 1e-5

L0, L1, L2, L2T, L3 = range(5)
LAYER = [0, 1, 2, 2, 3]


def visits():
    out = []
    for i in range(NG):
        out += [(i, j, [], "rows") for j in range(i, NG)]
        out += [(i, j, [L0], "rows") for j in range(i)]
    out += [(2, 2, [L0], "cols"), (3, 3, [L0], "cols"), (2, 3, [L0], "cols"),
            (1, 1, [L0], "cols"), (1, 3, [L0, L1], "cols"), (1, 2, [L0, L1], "cols"),
            (0, 3, [L0, L1], "cols"), (0, 2, [L0, L1], "cols"), (0, 1, [L0, L1], "cols"), (0, 0, [L0], "cols")]
    out += [(1, 1, [L1], ""), (0, 0, [L1], ""), (1, 0, [L1], "cols"),
            (2, 1, [L1], "cols"), (2, 3, [L1], ""), (2, 2, [L1], ""), (2, 0, [L1, L2], "cols"),
            (3, 2, [L1], "cols"), (3, 0, [L1, L2], "cols"), (3, 1, [L1, L2], "cols"), (3, 3, [L1], "")]
    out += [(3, 0, [L2T], ""), (3, 1, [L2T], ""), (3, 2, [L2T], ""), (3, 2, [L2], ""), (3, 3, [L2T], ""),
            (3, 3, [L2], "")]
    out += [(2, j, [L2T], "") for j in range(NG)] + [(2, 1, [L2], ""), (2, 2, [L2], ""), (2, 3, [L2, L3], "")]
    out += [(1, j, [L2T], "") for j in range(NG)] + [(1, 3, [L2, L3], ""), (1, 2, [L2, L3], ""),
                                                     (1, 0, [L2], ""), (1, 1, [L2], "")]
    out += [(0, j, [L2T], "") for j in range(NG)] + [(0, 3, [L2, L3], ""), (0, 2, [L2, L3], ""),
                                                     (0, 1, [L2, L3], ""), (0, 0, [L2], "")]
    out += [(3, 3, [L3], ""), (3, 2, [L3], ""), (3, 1, [L3], ""), (3, 0, [L3], "")]
    out += [(2, 0, [L3], ""), (2, 1, [L3], ""), (2, 2, [L3], ""), (1, 0, [L3], ""), (1, 1, [L3], ""), (0, 0, [L3], "")]
    return out


VISITS = visits()
for _p in (L0, L1, L2, L2T, L3):
    assert sorted((g, j) for g, j, ps, _ in VISITS if _p in ps) == [(g, j) for g in range(NG) for j in range(NG)]
assert sorted((g, j) for g, j, _, s in VISITS if s == "cols") == [(g, j) for g in range(NG) for j in range(NG)]
SWEEP = NG * NG
UNITS = len(VISITS) * VU

PASS_ENDS = (SWEEP, SWEEP + 10, SWEEP + 21, len(VISITS) - 10, len(VISITS))


class Run:

    def __init__(self, p, g, first):
        self.p, self.g, self.first, self.last = p, g, first, first

    @property
    def closed(self):
        return (self.last + 1) * VU


def runs():
    out, open_run = [], {}
    for v, (g, _, products, _) in enumerate(VISITS):
        stage = sum(v >= end for end in PASS_ENDS)
        for p in products:
            if (p, g, stage) not in open_run:
                open_run[p, g, stage] = Run(p, g, v)
                out.append(open_run[p, g, stage])
            open_run[p, g, stage].last = v
    for r in out:
        same = [s for s in out if (s.p, s.g) == (r.p, r.g)]
        r.final = r is same[-1]
        r.has_partial = r.final and len(same) > 1
    freed = [-1, -1]
    before = [None, None]
    for v in range(len(VISITS)):
        for r in [r for r in out if r.first == v]:
            r.bank = min((0, 1), key=lambda b: freed[b])
            assert freed[r.bank] < v
            r.before = before[r.bank]
            before[r.bank], freed[r.bank] = r, r.last
    return out


RUNS = runs()

TURN_AT, PROJECT_AT = 0, 1
MSG_AT, GATES_AT, MIX_AT = (1, 6), (3, 8), (7, 12)
TAKE_AT, SCALE_AT, APPLY_AT = 2, 4, 5
ACT_MSG_AT, ACT_GATES_AT, ACT_NEW_AT, GRU_APPLY_AT = (4, 9), (7, 12), (8, 13), 15
RESIDUAL_AT, LOW_AT = 4, 6
DVE_NEW_AT, DVE_MIX_AT, DVE_GRU_AT, GRU_LOW_AT = (7, 12), (8, 13), (10, 14), 16
SPAN = {L0: 4, L1: 12, L2: 4, L2T: 4, L3: 4}
TAIL = 18


class Epilogue:

    def __init__(self, run, start):
        self.run, self.p, self.g, self.start = run, run.p, run.g, start
        run.epilogue = self


def epilogues():
    out, free = [], 0
    for r in sorted((r for r in RUNS if r.final), key=lambda r: (r.last, r.p)):
        out.append(Epilogue(r, max(r.closed, free)))
        free = out[-1].start + SPAN[r.p]
    return out


EPILOGUES = epilogues()


def before(e, products):
    return sum(x.p in products for x in EPILOGUES[:EPILOGUES.index(e)])


PROJ = (L0, L2, L2T, L3)
SELF = (L0, L1, L3)
NORM = (L0, L1, L2)

NORM_OF = {(0, g): g for g in range(NG)}
for _e in EPILOGUES:
    if _e.p in NORM:
        NORM_OF[LAYER[_e.p] + 1, _e.g] = NG + before(_e, NORM)

SPLIT_NO = {}
for _u in range(UNITS):
    if VISITS[_u // VU][2]:
        SPLIT_NO[_u] = len(SPLIT_NO)


def splits_before(unit):
    return sum(u < unit for u in SPLIT_NO)


def takes(on_vector):
    out = {}
    for r in sorted(RUNS, key=lambda r: (take_unit(r), r.last, not r.final, r.p)):
        if r.has_partial == on_vector:
            out[r] = len(out)
    return out


def take_unit(r):
    return (r.epilogue.start if r.final and r.p != L1 else r.closed) + TAKE_AT


ACT_TAKES, DVE_TAKES = takes(False), takes(True)

W0, WMSG, WIH, WHH, WIN, WOUT, W3 = 0, 1, 2, 5, 8, 9, 10
NPAR = 11
WEIGHT = {L0: W0, L2: WIN, L2T: WOUT, L3: W3}
BR0, BR3 = 0, 1
BMSG, BIH, BHH = 0, 1, 4
NCOL = 7


def build_gnn(nc, x_in, a_rows, a_cols, params, rows, alpha, out):
    F32, F32R = mybir.dt.float32, mybir.dt.float32r
    ACT = mybir.ActivationFunctionType
    ALU = mybir.AluOpType
    AX = mybir.AxisListType

    ctx = ExitStack()
    with ctx:
        def sb(name, shape, dt=F32):
            return ctx.enter_context(nc.sbuf_tensor(name, shape, dt))

        def sem(name):
            return ctx.enter_context(nc.semaphore(name))

        raw = sb("raw", [P, RAW, JB * GC])
        a_high = sb("a_high", [P, SPLIT, JB * GC], F32R)
        a_low = sb("a_low", [P, SPLIT, JB * GC], F32R)
        x = sb("x", [P, NB, F])
        h_high = [sb(f"h_high{i}", [P, NB, F], F32R) for i in range(2)]
        h_low = [sb(f"h_low{i}", [P, NB, F], F32R) for i in range(2)]
        partial = [sb(f"partial{i}", [P, GC]) for i in range(NG)]
        par = sb("par", [P, NPAR * P + NCOL])
        cols = par[:, NPAR * P:]
        brow = sb("brow", [P, 2, F])
        alpha_col = sb("alpha_col", [P, 1])
        ybuf = sb("ybuf", [P, 2 * GC])
        y = ybuf[:, 0:GC]
        hsT = ybuf[:, GC:2 * GC]
        work = sb("work", [P, 2 * GC])
        tn = work[:, 0:GC]
        upd = work[:, GC:2 * GC]
        rrow = work[0:1, GC:2 * GC]
        msgT, gate_r, gate_z, new_n = (work[:, i * BANK:(i + 1) * BANK] for i in range(4))
        ident = sb("ident", [P, P])
        ident_r = sb("ident_r", [P, P], F32R)
        ones = sb("ones", [P, P])
        ones_r = sb("ones_r", [P, P], F32R)
        rsum = sb("rsum", [P, NB])
        csum = sb("csum", [P, NB])
        cpart = sb("cpart", [P, NG, NB])
        scale = {p: sb(f"scale{p}", [P, NB]) for p in PROJ}
        flag = sb("flag", [P, 2, NB])
        gbias = sb("gbias", [P, 2])
        one_m_a = sb("one_m_a", [P, 1])
        stats = sb("stats", [P, GB, 6])
        mv = sb("mv", [P, GB, 2])
        veps = sb("veps", [P, GB])
        rstd = sb("rstd", [P, GB])
        rscale = sb("rscale", [P, GB])
        shift = sb("shift", [P, GB])
        mhalf = sb("mhalf", [P, GB])
        dplus = sb("dplus", [P, GB])
        dgrp = sb("dgrp", [P, GB])

        acc = ctx.enter_context(nc.psum_tensor("acc", [P, 2, GC], F32))
        E = ctx.enter_context(nc.psum_tensor("E", [P, 4, BANK], F32))

        def bank(i):
            return E[:, i, :]

        def banks(i):
            return E[:, i:i + 2, :].rearrange("p a b -> p (a b)")

        def w(i):
            return par[:, bass.ts(i, P)]

        def group(t, g):
            return t[:, g * GB:(g + 1) * GB, :]

        def blocks(flat):
            return flat.rearrange("p (b f) -> p b f", f=F)

        def partial_of(p, g):
            return partial[g - 2 if p == L2 else g]

        x_loaded = sem("x_loaded")
        params_in = sem("params_in")
        rows_in = sem("rows_in")
        consts = sem("consts")
        rounded = sem("rounded")
        landed = [sem(f"landed{i}") for i in range(RAW)]
        act_unit = sem("act_unit")
        dve_unit = sem("dve_unit")
        pe_unit = sem("pe_unit")
        act_take = sem("act_take")
        dve_take = sem("dve_take")
        rows_folded = sem("rows_folded")
        row_done = sem("row_done")
        row_copied = sem("row_copied")
        row_spread = sem("row_spread")
        rows_saved = sem("rows_saved")
        d_ready = sem("d_ready")
        small = sem("small")
        degrees_done = sem("degrees_done")
        stats_done = sem("stats_done")
        moments = sem("moments")
        var_ready = sem("var_ready")
        rstd_ready = sem("rstd_ready")
        rscale_ready = sem("rscale_ready")
        shift_ready = sem("shift_ready")
        normed = sem("normed")
        high_ready = sem("high_ready")
        h_ready = sem("h_ready")
        bias_added = sem("bias_added")
        self_turned = sem("self_turned")
        selfT_ready = sem("selfT_ready")
        projected = sem("projected")
        scaled = sem("scaled")
        biased = sem("biased")
        x_new = sem("x_new")
        msg_done = sem("msg_done")
        msg_ready = sem("msg_ready")
        gates_done = sem("gates_done")
        r_ready = sem("r_ready")
        z_ready = sem("z_ready")
        reset_done = sem("reset_done")
        new_sum = sem("new_sum")
        n_ready = sem("n_ready")
        mixing = sem("mixing")
        mixed = sem("mixed")
        mix_turned = sem("mix_turned")
        x_gru = sem("x_gru")
        stored = sem("stored")

        def wait(eng, semaphore, count):
            if count > 0:
                eng.wait_ge(semaphore, count)

        def sum_taken(eng, run):
            if run.has_partial:
                wait(eng, dve_take, DVE_TAKES[run] + 1)
            else:
                wait(eng, act_take, ACT_TAKES[run] + 1)

        def final_run(p, g):
            return next(r for r in RUNS if (r.p, r.g) == (p, g) and r.final)

        def partial_free(eng, r):
            if r.p == L1 and not r.has_partial and (r.g > 0 or r.final):
                if r.g > 0:
                    sum_taken(eng, final_run(L0, r.g))
            elif r.p == L2:
                wait(eng, msg_done, CH * (r.g - 2 + 1))
            elif r.p == L3 and r.g == 2:
                wait(eng, msg_done, CH * 3)
            elif r.p == L3:
                sum_taken(eng, final_run(L2, 3 if r.g == 1 else 2))

        def workspace_free(eng, e):
            wait(eng, rows_folded, NG)
            wait(eng, projected, before(e, PROJ))
            wait(eng, mixed, CH * before(e, (L1,)))

        block = ctx.enter_context(nc.Block())

        @block.sync
        def _(sp):
            for unit in range(UNITS):
                g, j, products, _ = VISITS[unit // VU]
                source = a_cols if products == [L2T] else a_rows
                wait(sp, dve_unit, unit - RAW + 1)
                sp.dma_start(raw[:, unit % RAW, :], source[g * NU + j * VU + unit % VU])\
                    .then_inc(landed[unit % RAW], 16)
                if unit == RAW:
                    sp.dma_start(x[:, :, :], x_in.rearrange("(b p) f -> p b f", p=P)).then_inc(x_loaded, 16)
                    sp.dma_start(par[:, :], params).then_inc(params_in, 16)
                    for r in range(2):
                        sp.dma_start(brow[:, r, :], rows[r:r + 1, :].partition_broadcast(P)).then_inc(rows_in, 16)
                    sp.dma_start(alpha_col[:, :], alpha.partition_broadcast(P)).then_inc(rows_in, 16)
            for e in EPILOGUES:
                if e.p == L3:
                    sp.wait_ge(x_new, before(e, PROJ) + 1)
                    sp.dma_start(out.rearrange("(b p) f -> p b f", p=P)[:, e.g * GB:(e.g + 1) * GB, :],
                                 group(x, e.g)).then_inc(stored, 16)
            sp.wait_ge(stored, 16 * NG)

        @block.gpsimd
        def _(pool):
            nc.gpsimd.memset(ones[:, :], 1.0).then_inc(consts, 1)
            nc.gpsimd.memset(mhalf[:, :], -0.5).then_inc(consts, 1)
            nc.gpsimd.memset(ident[:, :], 0.0).then_inc(consts, 1)
            pool.wait_ge(consts, 3)
            nc.gpsimd.affine_select(out=ident[:, :], in_=ident[:, :], compare_op=ALU.not_equal, fill=1.0,
                                    base=0, pattern=[[-1, P]], channel_multiplier=1).then_inc(consts, 1)

            def reciprocal_std(k):
                pool.wait_ge(var_ready, k + 1)
                nc.gpsimd.tensor_tensor(rstd[:, :], veps[:, :], mhalf[:, :], ALU.pow).then_inc(rstd_ready, 1)

            for g in range(NG):
                reciprocal_std(g)
                pool.wait_ge(rows_saved, g + 1)
                nc.gpsimd.tensor_tensor(dgrp[:, :], dplus[:, :], mhalf[:, :], ALU.pow).then_inc(d_ready, 1)
            with pool.Fori(NG, len(NORM_OF)) as k:
                reciprocal_std(k)

        @block.scalar
        def _(act):
            act.wait_ge(consts, 4)
            nc.scalar.copy(ones_r[:, :], ones[:, :]).then_inc(rounded, 1)
            nc.scalar.copy(ident_r[:, :], ident[:, :]).then_inc(rounded, 1)

            def normalize(k, layer, g):
                act.wait_ge(shift_ready, k + 1)
                wait(act, h_ready, k)
                for b in range(GB):
                    last = nc.scalar.activation(tn[:, bass.ts(b, F)], x[:, g * GB + b, :], ACT.Relu,
                                                scale=rscale[:, b:b + 1], bias=shift[:, b:b + 1])
                last.then_inc(normed, 1)
                act.wait_ge(normed, k + 1)
                nc.scalar.copy(group(h_high[layer % 2], g), blocks(tn)).then_inc(high_ready, 1)

            def take(r):
                act.wait_ge(pe_unit, splits_before(r.closed))
                if r.final and r.p != L1:
                    workspace_free(act, r.epilogue)
                    target = hsT if r.p == L2 else y
                else:
                    partial_free(act, r)
                    target = partial_of(r.p, r.g)[:, :]
                if r.p == L3:
                    nc.scalar.activation(target, acc[:, r.bank, :], ACT.Copy, scale=alpha_col[:, 0:1])\
                        .then_inc(act_take, 1)
                else:
                    nc.scalar.copy(target, acc[:, r.bank, :]).then_inc(act_take, 1)

            def take_self(e):
                act.wait_ge(self_turned, before(e, SELF) + 1)
                workspace_free(act, e)
                if e.p == L3:
                    nc.scalar.activation(hsT, banks(2), ACT.Copy, scale=one_m_a[:, 0:1]).then_inc(selfT_ready, 1)
                else:
                    nc.scalar.copy(hsT, banks(2)).then_inc(selfT_ready, 1)

            def scale_projection(e):
                v = before(e, PROJ)
                act.wait_ge(projected, v + 1)
                wait(act, x_new, v)
                act.wait_ge(degrees_done, 2 if e.p == L2T else 1)
                for b in range(GB):
                    last = nc.scalar.activation(upd[:, bass.ts(b, F)], bank(b // CB)[:, bass.ts(b % CB, P)], ACT.Copy,
                                                scale=scale[e.p][:, e.g * GB + b:e.g * GB + b + 1])
                last.then_inc(scaled, 1)

            def message(e, q):
                act.wait_ge(msg_done, q + 1)
                wait(act, gates_done, q)
                act.wait_ge(h_ready, NG + before(e, NORM))
                nc.scalar.activation(msgT, bank(1), ACT.Relu, bias=cols[:, BMSG:BMSG + 1]).then_inc(msg_ready, 1)

            def gates(q):
                act.wait_ge(gates_done, q + 1)
                nc.scalar.activation(gate_r, bank(2), ACT.Sigmoid, bias=gbias[:, 0:1]).then_inc(r_ready, 1)
                nc.scalar.activation(gate_z, bank(3), ACT.Sigmoid, bias=gbias[:, 1:2]).then_inc(z_ready, 1)

            def new_state(q):
                act.wait_ge(new_sum, q + 1)
                nc.scalar.activation(new_n, new_n, ACT.Tanh, bias=cols[:, BIH + 2:BIH + 3]).then_inc(n_ready, 1)

            def epilogue(e, at):
                if at == TAKE_AT and e.p in SELF:
                    take_self(e)
                if at == SCALE_AT and e.p in PROJ:
                    scale_projection(e)
                if e.p == L1:
                    for c in range(CH):
                        q = CH * before(e, (L1,)) + c
                        if at == ACT_MSG_AT[c]:
                            message(e, q)
                        if at == ACT_GATES_AT[c]:
                            gates(q)
                        if at == ACT_NEW_AT[c]:
                            new_state(q)
                if e.p in NORM and at == (GRU_APPLY_AT if e.p == L1 else APPLY_AT):
                    normalize(NG + before(e, NORM), LAYER[e.p] + 1, e.g)

            for unit in range(UNITS + TAIL):
                for r in ACT_TAKES:
                    if take_unit(r) == unit:
                        take(r)
                for e in EPILOGUES:
                    epilogue(e, unit - e.start)
                for g in range(NG):
                    if unit == (g + 1) * NU + ROW_APPLY_AT:
                        normalize(g, 0, g)
                if unit not in SPLIT_NO:
                    continue
                g, j, _, sums = VISITS[unit // VU]
                s = SPLIT_NO[unit]
                act.wait_ge(landed[unit % RAW], 16 * (unit // RAW + 1))
                wait(act, pe_unit, s - SPLIT + 1)
                if sums == "cols":
                    for jb in range(JB):
                        b = j * GB + unit % VU * JB + jb
                        last = nc.scalar.activation(a_high[:, s % SPLIT, bass.ts(jb, GC)],
                                                    raw[:, unit % RAW, bass.ts(jb, GC)], ACT.Copy,
                                                    accum_out=cpart[:, g, b:b + 1])
                    last.then_inc(act_unit, 1)
                else:
                    nc.scalar.copy(a_high[:, s % SPLIT, :], raw[:, unit % RAW, :]).then_inc(act_unit, 1)

        @block.vector
        def _(dve):
            done = [0]

            def step(ins):
                done[0] += 1
                ins.then_inc(small, 1)
                dve.wait_ge(small, done[0])

            def statistics(k, g):
                wait(dve, h_ready, k)
                for b in range(GB):
                    last = nc.vector.bn_stats(stats[:, b, :], x[:, g * GB + b, :])
                last.then_inc(stats_done, 1)
                dve.wait_ge(stats_done, k + 1)
                for b in range(GB):
                    last = nc.vector.bn_aggr(mv[:, b, :], stats[:, b, :])
                last.then_inc(moments, 1)
                dve.wait_ge(moments, k + 1)
                nc.vector.tensor_scalar(veps[:, :], mv[:, :, 1], EPS, None, ALU.add).then_inc(var_ready, 1)

            def scale_and_shift(k, g):
                dve.wait_ge(rstd_ready, k + 1)
                if k < NG:
                    dve.wait_ge(d_ready, g + 1)
                    nc.vector.tensor_tensor(rscale[:, :], rstd[:, :], dgrp[:, :], ALU.mult).then_inc(rscale_ready, 1)
                else:
                    nc.vector.tensor_copy(rscale[:, :], rstd[:, :]).then_inc(rscale_ready, 1)
                dve.wait_ge(rscale_ready, k + 1)
                nc.vector.scalar_tensor_tensor(out=shift[:, :], in0=mv[:, :, 0], scalar=-1.0, in1=rscale[:, :],
                                               op0=ALU.mult, op1=ALU.mult).then_inc(shift_ready, 1)

            def low_part(k, layer, g):
                dve.wait_ge(high_ready, k + 1)
                nc.vector.tensor_tensor(group(h_low[layer % 2], g), blocks(tn),
                                        group(h_high[layer % 2], g).bitcast(F32), ALU.subtract).then_inc(h_ready, 1)

            def take(r):
                dve.wait_ge(pe_unit, splits_before(r.closed))
                if r.p == L1:
                    target = partial[r.g][:, :]
                else:
                    workspace_free(dve, r.epilogue)
                    target = hsT if r.p == L2 else y
                saved = next(s for s in RUNS if (s.p, s.g) == (r.p, r.g))
                dve.wait_ge(act_take, ACT_TAKES[saved] + 1)
                if r.p == L3:
                    nc.vector.scalar_tensor_tensor(out=target, in0=acc[:, r.bank, :], scalar=alpha_col[:, 0:1],
                                                   in1=partial_of(r.p, r.g)[:, :], op0=ALU.mult, op1=ALU.add)\
                        .then_inc(dve_take, 1)
                else:
                    nc.vector.tensor_tensor(target, acc[:, r.bank, :], partial_of(r.p, r.g)[:, :], ALU.add)\
                        .then_inc(dve_take, 1)

            def degrees():
                dve.wait_ge(rows_in, 48)
                dve.wait_ge(params_in, 16)
                a = alpha_col[:, 0:1]
                step(nc.vector.tensor_tensor(gbias[:, :], cols[:, BIH:BIH + 2], cols[:, BHH:BHH + 2], ALU.add))
                step(nc.vector.tensor_scalar(one_m_a[:, :], a, -1.0, 1.0, ALU.mult, ALU.add))
                deg, sc = scale[L3], scale[L3]
                step(nc.vector.tensor_scalar(deg[:, :], rsum[:, :], a, one_m_a[:, 0:1], ALU.mult, ALU.add))
                step(nc.vector.tensor_scalar(flag[:, 1, :], deg[:, :], 0.0, None, ALU.is_equal))
                step(nc.vector.tensor_tensor(flag[:, 0, :], deg[:, :], flag[:, 1, :], ALU.add))
                step(nc.vector.reciprocal(deg[:, :], flag[:, 0, :]))
                step(nc.vector.tensor_scalar(flag[:, 1, :], flag[:, 1, :], -1.0, 1.0, ALU.mult, ALU.add))
                step(nc.vector.tensor_tensor(sc[:, :], deg[:, :], flag[:, 1, :], ALU.mult))
                guarded_reciprocal(rsum, scale[L2])

            def guarded_reciprocal(deg, sc):
                step(nc.vector.tensor_scalar(flag[:, 0, :], deg[:, :], 0.0, None, ALU.is_gt))
                step(nc.vector.tensor_scalar(flag[:, 1, :], flag[:, 0, :], -1.0, 1.0, ALU.mult, ALU.add))
                step(nc.vector.tensor_tensor(flag[:, 0, :], flag[:, 0, :], deg[:, :], ALU.mult))
                step(nc.vector.tensor_tensor(flag[:, 0, :], flag[:, 0, :], flag[:, 1, :], ALU.add))
                nc.vector.reciprocal(sc[:, :], flag[:, 0, :]).then_inc(degrees_done, 1)

            def column_degrees():
                dve.wait_ge(act_unit, splits_before(COLUMNS_DONE))
                dve.wait_ge(degrees_done, 1)
                step(nc.vector.tensor_reduce(csum[:, :], cpart[:, :, :].rearrange("p g b -> p b g"), AX.X, ALU.add))
                guarded_reciprocal(csum, scale[L2T])

            def sweep_steps(g, at):
                if at == 0:
                    if g == 0:
                        dve.wait_ge(x_loaded, 16)
                        dve.wait_ge(rows_in, 48)
                    statistics(g, g)
                if at == ROW_COPY_AT:
                    dve.wait_ge(rows_folded, g + 1)
                    wait(dve, row_done, g)
                    nc.vector.tensor_copy(rrow, E[0:1, 0:2, :].rearrange("p a b -> p (a b)")).then_inc(row_copied, 1)
                if at == ROW_SAVE_AT:
                    dve.wait_ge(row_spread, g + 1)
                    nc.vector.tensor_copy(rsum[:, bass.ts(g, GB)], bank(2)[:, 0:GB])
                    nc.vector.tensor_scalar(dplus[:, :], bank(2)[:, 0:GB], 1.0, None, ALU.add).then_inc(rows_saved, 1)
                if at == ROW_APPLY_AT:
                    scale_and_shift(g, g)
                    nc.vector.tensor_copy(scale[L0][:, bass.ts(g, GB)], dgrp[:, :])
                if at == ROW_LOW_AT:
                    low_part(g, 0, g)
                    nc.vector.tensor_tensor(group(x, g), group(x, g),
                                            brow[:, BR0, :].unsqueeze(1).to_broadcast([P, GB, F]), ALU.add)\
                        .then_inc(bias_added, 1)

            def residual(e):
                v = before(e, PROJ)
                xg = group(x, e.g)
                dve.wait_ge(scaled, v + 1)
                if e.p == L0:
                    dve.wait_ge(bias_added, e.g + 1)
                if e.p == L3:
                    nc.vector.tensor_tensor(blocks(upd), blocks(upd),
                                            brow[:, BR3, :].unsqueeze(1).to_broadcast([P, GB, F]), ALU.add)\
                        .then_inc(biased, 1)
                    dve.wait_ge(biased, before(e, (L3,)) + 1)
                    nc.vector.scalar_tensor_tensor(out=xg, in0=blocks(upd), scalar=0.0, in1=xg,
                                                   op0=ALU.max, op1=ALU.add).then_inc(x_new, 1)
                else:
                    nc.vector.tensor_tensor(xg, xg, blocks(upd), ALU.add).then_inc(x_new, 1)
                dve.wait_ge(x_new, v + 1)

            def new_state(q):
                dve.wait_ge(r_ready, q + 1)
                nc.vector.scalar_tensor_tensor(out=new_n, in0=bank(0), scalar=cols[:, BHH + 2:BHH + 3], in1=gate_r,
                                               op0=ALU.add, op1=ALU.mult).then_inc(reset_done, 1)
                dve.wait_ge(reset_done, q + 1)
                nc.vector.tensor_tensor(new_n, new_n, bank(1), ALU.add).then_inc(new_sum, 1)

            def mix(q, c):
                dve.wait_ge(n_ready, q + 1)
                nc.vector.tensor_tensor(gate_r, hsT[:, bass.ts(c, BANK)], new_n, ALU.subtract).then_inc(mixing, 1)
                dve.wait_ge(mixing, 2 * q + 1)
                nc.vector.tensor_tensor(gate_r, gate_r, gate_z, ALU.mult).then_inc(mixing, 1)
                dve.wait_ge(mixing, 2 * q + 2)
                nc.vector.tensor_tensor(gate_r, gate_r, new_n, ALU.add).then_inc(mixed, 1)

            def gru_residual(q, g, c):
                xc = x[:, g * GB + c * CB:g * GB + (c + 1) * CB, :]
                dve.wait_ge(mix_turned, q + 1)
                nc.vector.tensor_tensor(xc, xc, blocks(bank(2)), ALU.add).then_inc(x_gru, 1)

            def epilogue(e, at):
                if e.p in PROJ and at == RESIDUAL_AT:
                    residual(e)
                if e.p == L1:
                    for c in range(CH):
                        q = CH * before(e, (L1,)) + c
                        if at == DVE_NEW_AT[c]:
                            new_state(q)
                        if at == DVE_MIX_AT[c]:
                            mix(q, c)
                        if at == DVE_GRU_AT[c]:
                            gru_residual(q, e.g, c)
                if e.p in NORM:
                    k = NG + before(e, NORM)
                    if at == (DVE_GRU_AT[-1] if e.p == L1 else RESIDUAL_AT):
                        if e.p == L1:
                            dve.wait_ge(x_gru, CH * (before(e, (L1,)) + 1))
                        statistics(k, e.g)
                        scale_and_shift(k, e.g)
                    if at == (GRU_LOW_AT if e.p == L1 else LOW_AT):
                        low_part(k, LAYER[e.p] + 1, e.g)

            for unit in range(UNITS + TAIL):
                for r in DVE_TAKES:
                    if take_unit(r) == unit:
                        take(r)
                for e in EPILOGUES:
                    epilogue(e, unit - e.start)
                for g in range(NG):
                    sweep_steps(g, unit - (g + 1) * NU)
                if unit == SWEEP * VU + 8:
                    degrees()
                if unit == COLUMNS_DONE + SPLIT:
                    column_degrees()
                if unit >= UNITS:
                    continue
                g, j, products, _ = VISITS[unit // VU]
                new = raw[:, unit % RAW, :]
                dve.wait_ge(landed[unit % RAW], 16 * (unit // RAW + 1))
                if products:
                    s = SPLIT_NO[unit]
                    dve.wait_ge(act_unit, s + 1)
                    wait(dve, pe_unit, s - SPLIT + 1)
                    nc.vector.tensor_tensor(a_low[:, s % SPLIT, :], new, a_high[:, s % SPLIT, :].bitcast(F32),
                                            ALU.subtract).then_inc(dve_unit, 1)
                elif unit % NU == 0:
                    wait(dve, rows_folded, g)
                    nc.vector.tensor_copy(ybuf[:, :], new).then_inc(dve_unit, 1)
                else:
                    dve.wait_ge(dve_unit, unit)
                    nc.vector.tensor_tensor(ybuf[:, :], ybuf[:, :], new, ALU.add).then_inc(dve_unit, 1)

        @block.tensor
        def _(pe):
            pe.wait_ge(consts, 4)
            pe.wait_ge(rounded, 2)

            def fold_rows(g):
                pe.wait_ge(dve_unit, g * NU + (NG - g) * VU)
                wait(pe, row_copied, g)
                for c in range(CH):
                    for jb in range(JB):
                        last = nc.tensor.matmul(bank(c), ones[:, :], ybuf[:, jb * GC + c * BANK:jb * GC + (c + 1) * BANK],
                                                start=jb == 0, stop=g == 0 and jb == JB - 1)
                last.then_inc(rows_folded, 1)

            def spread_rows(g):
                pe.wait_ge(row_copied, g + 1)
                wait(pe, rows_saved, g)
                for b in range(GB):
                    last = nc.tensor.matmul(bank(2)[:, b:b + 1], rrow[:, bass.ts(b, P)], ones[0:1, 0:1],
                                            start=True, stop=True)
                last.then_inc(row_spread, 1)

            def turn_self(e):
                layer = LAYER[e.p]
                pe.wait_ge(rows_saved, NG)
                wait(pe, selfT_ready, before(e, SELF))
                wait(pe, z_ready, CH * before(e, (L1,)))
                wait(pe, x_gru, CH * before(e, (L1,)))
                for b in range(GB):
                    for part in (h_high, h_low):
                        last = nc.tensor.matmul(bank(2 + b // CB)[:, bass.ts(b % CB, P)],
                                                part[layer % 2][:, e.g * GB + b, :], ident_r[:, :],
                                                start=part is h_high, stop=part is h_low)
                last.then_inc(self_turned, 1)

            def project(e):
                sum_taken(pe, e.run)
                wait(pe, scaled, before(e, PROJ))
                wait(pe, new_sum, CH * before(e, (L1,)))
                pe.wait_ge(row_copied, NG)
                own = e.p in SELF
                if own:
                    pe.wait_ge(selfT_ready, before(e, SELF) + 1)
                source = hsT if e.p == L2 else y
                for b in range(GB):
                    o = bank(b // CB)[:, bass.ts(b % CB, P)]
                    last = nc.tensor.matmul(o, source[:, bass.ts(b, P)], w(WEIGHT[e.p]), start=True, stop=not own)
                    if own:
                        last = nc.tensor.matmul(o, hsT[:, bass.ts(b, P)], w(WEIGHT[e.p]), start=False, stop=True)
                last.then_inc(projected, 1)

            def message(e, q, c):
                sum_taken(pe, e.run)
                pe.wait_ge(scaled, before(e, PROJ))
                wait(pe, new_sum, q)
                nc.tensor.matmul(bank(1), w(WMSG), partial[e.g][:, bass.ts(c, BANK)], start=True, stop=True)\
                    .then_inc(msg_done, 1)

            def gates(e, q, c):
                m, h = msgT, hsT[:, bass.ts(c, BANK)]
                pe.wait_ge(selfT_ready, before(e, SELF) + 1)
                pe.wait_ge(msg_ready, q + 1)
                wait(pe, x_gru, q)
                for i in range(2):
                    nc.tensor.matmul(bank(2 + i), w(WIH + i), m, start=True, stop=False)
                    nc.tensor.matmul(bank(2 + i), w(WHH + i), h, start=False, stop=True)
                nc.tensor.matmul(bank(0), w(WHH + 2), h, start=True, stop=True)
                nc.tensor.matmul(bank(1), w(WIH + 2), m, start=True, stop=True).then_inc(gates_done, 1)

            def turn_mix(q):
                pe.wait_ge(mixed, q + 1)
                for b in range(CB):
                    last = nc.tensor.transpose(bank(2)[:, bass.ts(b, P)], gate_r[:, bass.ts(b, P)], ident[:, :])
                last.then_inc(mix_turned, 1)

            def epilogue(e, at):
                if e.p in SELF and at == TURN_AT:
                    turn_self(e)
                if e.p in PROJ and at == PROJECT_AT:
                    project(e)
                if e.p == L1:
                    for c in range(CH):
                        q = CH * before(e, (L1,)) + c
                        if at == MSG_AT[c]:
                            message(e, q, c)
                        if at == MIX_AT[c]:
                            turn_mix(q)
                        if at == GATES_AT[c]:
                            gates(e, q, c)

            def multiply(unit):
                v, k = unit // VU, unit % VU
                g, j, products, sums = VISITS[v]
                s = SPLIT_NO[unit]
                slot = s % SPLIT
                mine = [r for r in RUNS if r.p in products and r.g == g and r.first <= v <= r.last]
                for r in mine:
                    if k == 0:
                        pe.wait_ge(h_ready, NORM_OF[LAYER[r.p], j] + 1)
                    if k == 0 and v == r.first and r.before is not None:
                        sum_taken(pe, r.before)
                pe.wait_ge(act_unit, s + 1)

                def column(jb, c):
                    return slice(jb * GC + c * BANK, jb * GC + (c + 1) * BANK)

                for r in mine:
                    high, low = h_high[LAYER[r.p] % 2], h_low[LAYER[r.p] % 2]
                    for jb in range(JB):
                        b = j * GB + k * JB + jb
                        for part in (high, low):
                            for c in range(CH):
                                nc.tensor.matmul(acc[:, r.bank, bass.ts(c, BANK)], part[:, b, :],
                                                 a_high[:, slot, column(jb, c)],
                                                 start=v == r.first and k == 0 and jb == 0 and part is high,
                                                 stop=False)
                last_of_row = sums == "rows" and unit % NU == NU - 1
                if sums == "rows":
                    for jb in range(JB):
                        for c in range(CH):
                            nc.tensor.matmul(bank(c), ones_r[:, :], a_high[:, slot, column(jb, c)],
                                             start=False, stop=False)
                pe.wait_ge(dve_unit, unit + 1)
                if sums == "rows":
                    for jb in range(JB):
                        for c in range(CH):
                            last = nc.tensor.matmul(bank(c), ones_r[:, :], a_low[:, slot, column(jb, c)],
                                                    start=False, stop=last_of_row and jb == JB - 1)
                    if last_of_row:
                        last.then_inc(row_done, 1)
                for r in mine:
                    for jb in range(JB):
                        b = j * GB + k * JB + jb
                        for c in range(CH):
                            last = nc.tensor.matmul(acc[:, r.bank, bass.ts(c, BANK)],
                                                    h_high[LAYER[r.p] % 2][:, b, :], a_low[:, slot, column(jb, c)],
                                                    start=False, stop=v == r.last and k == VU - 1 and jb == JB - 1)
                last.then_inc(pe_unit, 1)

            for unit in range(UNITS + TAIL):
                for g in range(NG):
                    if unit == g * NU + (NG - g) * VU:
                        fold_rows(g)
                    if unit == (g + 1) * NU:
                        spread_rows(g)
                if unit == SWEEP * VU:
                    pe.wait_ge(params_in, 16)
                for e in EPILOGUES:
                    epilogue(e, unit - e.start)
                if unit in SPLIT_NO:
                    multiply(unit)


ROW_COPY_AT, ROW_SAVE_AT, ROW_APPLY_AT, ROW_LOW_AT = 1, 2, 3, 4
COLUMNS_DONE = VU * (1 + max(v for v, x in enumerate(VISITS) if x[3] == "cols"))
def kernel(**inputs):
    import numpy as np
    import concourse.bacc as bacc
    from concourse.bass_utils import run_bass_kernel_spmd

    def tiles(a):
        return np.ascontiguousarray(
            a.reshape(NU, JB, P, NG, GC).transpose(3, 0, 2, 1, 4).reshape(NG * NU, P, JB * GC))

    a = {k: np.asarray(v) for k, v in inputs.items()}
    params = np.concatenate([
        a["L0_gnn_W"].T, a["L1_gnn_W_msg"].T, a["L1_gnn_W_ih"].T, a["L1_gnn_W_hh"].T, a["L2_gnn_W_in"],
        a["L2_gnn_W_out"], a["L3_gnn_W"].T, a["L1_gnn_b_msg"][:, None], a["L1_gnn_b_ih"].reshape(3, F).T,
        a["L1_gnn_b_hh"].reshape(3, F).T], axis=1)
    arrays = {
        "x_in": np.ascontiguousarray(a["x"]), "a_rows": tiles(a["adj"].T), "a_cols": tiles(a["adj"]),
        "params": np.ascontiguousarray(params), "rows": np.stack([a["L0_gnn_b"], a["L3_gnn_b"]]),
        "alpha": a["L3_gnn_alpha"].reshape(1, 1),
    }
    nc = bacc.Bacc("TRN2", target_bir_lowering=False, num_devices=1)
    f32 = mybir.dt.float32
    aps = {k: nc.dram_tensor(k, v.shape, f32, kind="ExternalInput").ap() for k, v in arrays.items()}
    out = nc.dram_tensor("out", (N, F), f32, kind="ExternalOutput").ap()
    build_gnn(nc, out=out, **aps)
    r = run_bass_kernel_spmd(nc, [arrays], core_ids=[0])
    return r.results[0]["out"]
```

```python
import concourse.bass as bass
from concourse import mybir
from contextlib import ExitStack

N = 4096
F = 128
P = 128
GC = 1024
NG = N // GC
GB = GC // P
NB = N // P
JB = 2
VU = GC // (JB * P)
NU = NB // JB
BANK = 512
CH = GC // BANK
CB = BANK // P
RAW = 4
SPLIT = 3
EPS = 1e-5

L0, L1, L2, L2T, L3 = range(5)
LAYER = [0, 1, 2, 2, 3]


SWEEP_ORDER = ("0R " * NU + "1R " * 6 + "10 1R " * VU + "1R " * 2 + "20 2R " * VU + "30 21 2R " * VU
               + "31 3R " * VU + "32 " * VU)


def sweep():
    rest = {i: [(j, k) for j in range(i, NG) for k in range(VU)] for i in range(NG)}
    shared = {(i, j): list(range(VU)) for i in range(NG) for j in range(i)}
    out = []
    for row, what in SWEEP_ORDER.split():
        i = int(row)
        if what == "R":
            out.append((i, *rest[i].pop(0), [], "rows"))
        else:
            out.append((i, int(what), shared[i, int(what)].pop(0), [L0], "rows"))
    return out


def visits():
    out = []
    out += [(2, 2, [L0], "cols"), (3, 3, [L0], "cols"), (2, 3, [L0], "cols"),
            (1, 1, [L0], "cols"), (1, 3, [L0, L1], "cols"), (1, 2, [L0, L1], "cols"),
            (0, 3, [L0, L1], "cols"), (0, 2, [L0, L1], "cols"), (0, 1, [L0, L1], "cols"), (0, 0, [L0], "cols")]
    out += [(3, 2, [L1], "cols"), (2, 1, [L1], "cols"), (0, 0, [L1], ""), (2, 3, [L1], ""), (1, 1, [L1], ""),
            (1, 0, [L1], "cols"), (2, 2, [L1], ""), (2, 0, [L1, L2], "cols"),
            (3, 0, [L1, L2], "cols"), (3, 3, [L1], ""), (3, 1, [L1, L2], "cols")]
    out += [(g, j, [L2T], "") for g, j in ((3, 0), (3, 1), (3, 2), (2, 0), (2, 1), (3, 3), (2, 2))]
    out += [(3, 2, [L2], ""), (3, 3, [L2], ""), (2, 3, [L2T], ""), (2, 1, [L2], ""), (2, 2, [L2], ""), (2, 3, [L2, L3], "")]
    out += [(1, j, [L2T], "") for j in range(NG)] + [(1, 3, [L2, L3], ""), (1, 2, [L2, L3], ""),
                                                     (1, 0, [L2], ""), (1, 1, [L2], "")]
    out += [(0, j, [L2T], "") for j in range(NG)] + [(0, 3, [L2, L3], ""), (0, 2, [L2, L3], ""),
                                                     (0, 1, [L2, L3], ""), (0, 0, [L2], "")]
    out += [(g, j, [L3], "") for g, j in ((3, 3), (3, 2), (3, 1), (1, 1), (3, 0), (1, 0), (0, 0),
                                          (2, 1), (2, 2), (2, 0))]
    return out


VISITS = visits()
SWEEP = len(sweep())
LOADS = sweep() + [(g, j, k, products, sums) for g, j, products, sums in VISITS for k in range(VU)]
UNITS = len(LOADS)
ALL = sorted((g, j, k) for g in range(NG) for j in range(NG) for k in range(VU))
for _p in (L0, L1, L2, L2T, L3):
    assert sorted((g, j, k) for g, j, k, ps, _ in LOADS if _p in ps) == ALL
for _kind in ("rows", "cols"):
    assert sorted((g, j, k) for g, j, k, _, sums in LOADS if sums == _kind) == ALL
COLUMNS_DONE = 1 + max(unit for unit, load in enumerate(LOADS) if load[4] == "cols")


ROW_END = [1 + max(u for u in range(SWEEP) if LOADS[u][0] == g) for g in range(NG)]
REST = [[u for u in range(SWEEP) if LOADS[u][0] == g and not LOADS[u][3]] for g in range(NG)]
REST_END = [units[-1] + 1 for units in REST]


def shared_before(g, unit):
    return sum(load[0] == g and bool(load[3]) for load in LOADS[:unit])


PASS_ENDS = [SWEEP] + [SWEEP + VU * visits for visits in (10, 21, len(VISITS) - 10, len(VISITS))]
SAVED_AFTER = {(L1, 3, 2)}


class Run:

    def __init__(self, p, g, first):
        self.p, self.g, self.first, self.last = p, g, first, first

    @property
    def closed(self):
        return self.last + 1


def runs():
    out, open_run = [], {}
    for v, (g, j, k, products, _) in enumerate(LOADS):
        stage = sum(v >= end for end in PASS_ENDS)
        for p in products:
            if (p, g, stage) not in open_run:
                open_run[p, g, stage] = Run(p, g, v)
                out.append(open_run[p, g, stage])
            open_run[p, g, stage].last = v
            if (p, g, j) in SAVED_AFTER and k == VU - 1:
                del open_run[p, g, stage]
    for r in out:
        same = [s for s in out if (s.p, s.g) == (r.p, r.g)]
        r.final = r is same[-1]
        r.has_partial = r.final and len(same) > 1
    freed = [-1, -1]
    before = [None, None]
    for v in range(UNITS):
        for r in [r for r in out if r.first == v]:
            r.bank = min((0, 1), key=lambda b: freed[b])
            assert freed[r.bank] < v
            r.before = before[r.bank]
            before[r.bank], freed[r.bank] = r, r.last
    return out


RUNS = runs()

TURN_AT, PROJECT_AT = {L0: -1, L1: 1, L3: -1}, {L0: 3, L2: 2, L2T: 2, L3: 3}
MSG_AT, GATES_AT, MIX_AT = 2, (4, 6), 11
TAKE_AT, SCALE_AT, HIGH_AT = 2, {L2: 5, L2T: 5, L3: 6}, {L0: 7, L1: 16, L2: 12}
ACT_NORM_AT = {L1: (16, 16), L2: (10, 11)}
ACT_MSG_AT, ACT_GATES_AT, ACT_NEW_AT = 4, (6, 9), (7, 10)
OWN_AT, ADD_OWN_AT = {L0: -2, L1: 1, L3: -2}, (3, 1)
RESIDUAL_AT = {L0: 5, L1: 13, L2: 6, L2T: 6, L3: 7}
STATS_AT, NORM_AT, LOW_AT = {L0: (5, 5), L1: (13, 14), L2: (7, 8)}, {L0: 6, L1: 15, L2: 9}, {L0: 8, L1: 17, L2: 13}
DVE_NEW_AT, DVE_MIX_AT = (6, 9), (8, 11)
ROW_STATS_AT, ROW_NORM_AT = -6, -5
ROW_COPY_AT, ROW_SPREAD_AT = (2, 2, 2, 1), (2, 2, 2, 1)
ROW_SAVE_AT, ROW_HIGH_AT, ROW_LOW_AT = (4, 4, 4, 2), (5, 5, 5, 3), (6, 6, 6, 4)
BIAS_AT = [SWEEP + at for at in (26, 24, -2, 3)]
SPAN = {L0: 4, L1: 11, L2: 4, L2T: 4, L3: 4}
TAIL = 19


class Epilogue:

    def __init__(self, run, start):
        self.run, self.p, self.g, self.start = run, run.p, run.g, start
        run.epilogue = self


def epilogues():
    out, free = [], 0
    for r in sorted((r for r in RUNS if r.final), key=lambda r: (r.last, r.p)):
        out.append(Epilogue(r, max(r.closed, free)))
        free = out[-1].start + SPAN[r.p]
    return out


EPILOGUES = epilogues()


def shifts_before(k):
    return sum(NORM_OF[LAYER[e.p] + 1, e.g] < k for e in EPILOGUES if e.p in ACT_NORMED)


def before(e, products):
    return sum(x.p in products for x in EPILOGUES[:EPILOGUES.index(e)])


PROJ = (L0, L2, L2T, L3)
SELF = (L0, L1, L3)
ACT_SCALED = (L2, L2T, L3)
ACT_NORMED = (L1, L2)
NORM = (L0, L1, L2)

NORM_OF = {(0, g): g for g in range(NG)}
for _e in EPILOGUES:
    if _e.p in NORM:
        NORM_OF[LAYER[_e.p] + 1, _e.g] = NG + before(_e, NORM)

SPLIT_NO = {}
for _u in range(UNITS):
    if LOADS[_u][3]:
        SPLIT_NO[_u] = len(SPLIT_NO)


def splits_before(unit):
    return sum(u < unit for u in SPLIT_NO)


def takes(on_vector):
    out = {}
    for r in sorted(RUNS, key=lambda r: (take_unit(r), r.last, not r.final, r.p)):
        if r.has_partial == on_vector:
            out[r] = len(out)
    return out


def take_unit(r):
    return (r.epilogue.start if r.final and r.p != L1 else r.closed) + TAKE_AT


ACT_TAKES, DVE_TAKES = takes(False), takes(True)

W0, WMSG, WIH, WHH, WIN, WOUT, W3 = 0, 1, 2, 5, 8, 9, 10
NPAR = 11
WEIGHT = {L0: W0, L2: WIN, L2T: WOUT, L3: W3}
BR0, BR3 = 0, 1
BMSG, BIH, BHH = 0, 1, 4
NCOL = 7


def build_gnn(nc, x_in, a_rows, a_cols, params, rows, alpha, out):
    F32, F32R = mybir.dt.float32, mybir.dt.float32r
    ACT = mybir.ActivationFunctionType
    ALU = mybir.AluOpType
    AX = mybir.AxisListType

    ctx = ExitStack()
    with ctx:
        def sb(name, shape, dt=F32):
            return ctx.enter_context(nc.sbuf_tensor(name, shape, dt))

        def sem(name):
            return ctx.enter_context(nc.semaphore(name))

        raw = sb("raw", [P, RAW, JB * GC])
        a_high = sb("a_high", [P, SPLIT, JB * GC], F32R)
        a_low = sb("a_low", [P, SPLIT, JB * GC], F32R)
        x = sb("x", [P, NB, F])
        h_high = [sb(f"h_high{i}", [P, NB, F], F32R) for i in range(2)]
        h_low = [sb(f"h_low{i}", [P, NB, F], F32R) for i in range(2)]
        partial = [sb(f"partial{i}", [P, GC]) for i in range(NG)]
        par = sb("par", [P, NPAR * P + NCOL])
        cols = par[:, NPAR * P:]
        brow = sb("brow", [P, 2, F])
        alpha_col = sb("alpha_col", [P, 1])
        ybuf = sb("ybuf", [P, 2 * GC])
        y = ybuf[:, 0:GC]
        hsT = ybuf[:, GC:2 * GC]
        work = sb("work", [P, 2 * GC])
        tn = work[:, 0:GC]
        upd = work[:, GC:2 * GC]
        rrow = work[0:1, GC:2 * GC]
        msgT = y
        gate_r = sb("gate_r", [P, BANK])[:, :]
        gate_z, new_n = (upd[:, i * BANK:(i + 1) * BANK] for i in range(2))
        ident = sb("ident", [P, P])
        ones = sb("ones", [P, P])
        ones_r = sb("ones_r", [P, P], F32R)
        rsum = sb("rsum", [P, NB])
        csum = sb("csum", [P, NB])
        cpart = sb("cpart", [P, NG, NB])
        scale = {p: sb(f"scale{p}", [P, NB]) for p in PROJ}
        flag = sb("flag", [P, 2, NB])
        gbias = sb("gbias", [P, 2])
        one_m_a = sb("one_m_a", [P, 1])
        stats = sb("stats", [P, GB, 6])
        mv = sb("mv", [P, GB, 2])
        veps = sb("veps", [P, GB])
        rstd = sb("rstd", [P, GB])
        shift = sb("shift", [P, GB])
        mhalf = sb("mhalf", [P, GB])
        dplus = sb("dplus", [P, GB])
        dgrp = sb("dgrp", [P, GB])

        acc = ctx.enter_context(nc.psum_tensor("acc", [P, 2, GC], F32))
        E = ctx.enter_context(nc.psum_tensor("E", [P, 4, BANK], F32))

        def bank(i):
            return E[:, i, :]

        def banks(i):
            return E[:, i:i + 2, :].rearrange("p a b -> p (a b)")

        def row_bank(g):
            return 2 * (g % 2)

        def w(i):
            return par[:, bass.ts(i, P)]

        def group(t, g):
            return t[:, g * GB:(g + 1) * GB, :]

        halves = [range(GB // 2), range(GB // 2, GB)]

        def blocks(flat):
            return flat.rearrange("p (b f) -> p b f", f=F)

        def partial_of(p, g):
            return partial[g - 2 if p == L2 else g]

        x_loaded = sem("x_loaded")
        params_in = sem("params_in")
        rows_in = sem("rows_in")
        consts = sem("consts")
        rounded = sem("rounded")
        landed = [sem(f"landed{i}") for i in range(RAW)]
        act_unit = sem("act_unit")
        dve_unit = sem("dve_unit")
        pe_unit = sem("pe_unit")
        act_take = sem("act_take")
        dve_take = sem("dve_take")
        rows_folded = sem("rows_folded")
        row_done = sem("row_done")
        row_copied = sem("row_copied")
        row_spread = sem("row_spread")
        rows_saved = sem("rows_saved")
        d_ready = sem("d_ready")
        small = sem("small")
        degrees_done = sem("degrees_done")
        stats_done = sem("stats_done")
        moments = sem("moments")
        var_ready = sem("var_ready")
        rstd_ready = sem("rstd_ready")
        weighted = sem("weighted")
        shift_ready = sem("shift_ready")
        normed = sem("normed")
        high_ready = sem("high_ready")
        h_ready = sem("h_ready")
        bias_added = sem("bias_added")
        own_ready = sem("own_ready")
        self_turned = sem("self_turned")
        self_added = sem("self_added")
        selfT_ready = sem("selfT_ready")
        projected = sem("projected")
        scaled = sem("scaled")
        biased = sem("biased")
        x_new = sem("x_new")
        msg_done = sem("msg_done")
        msg_ready = sem("msg_ready")
        gates_done = sem("gates_done")
        r_ready = sem("r_ready")
        z_ready = sem("z_ready")
        reset_done = sem("reset_done")
        new_sum = sem("new_sum")
        n_ready = sem("n_ready")
        mixing = sem("mixing")
        mixed = sem("mixed")
        mix_turned = sem("mix_turned")
        x_gru = sem("x_gru")
        stored = sem("stored")

        def wait(eng, semaphore, count):
            if count > 0:
                eng.wait_ge(semaphore, count)

        def sum_taken(eng, run):
            if run.has_partial:
                wait(eng, dve_take, DVE_TAKES[run] + 1)
            else:
                wait(eng, act_take, ACT_TAKES[run] + 1)

        def first_run(p, g):
            return next(r for r in RUNS if (r.p, r.g) == (p, g))

        def final_run(p, g):
            return next(r for r in RUNS if (r.p, r.g) == (p, g) and r.final)

        def partial_free(eng, r):
            if r.p == L1 and not r.has_partial and (r.g > 0 or r.final):
                if r.g > 0:
                    sum_taken(eng, final_run(L0, r.g))
            elif r.p == L2:
                wait(eng, msg_done, r.g - 2 + 1)
            elif r.p == L3 and r.g == 2:
                wait(eng, msg_done, 3)
            elif r.p == L3:
                sum_taken(eng, final_run(L2, 3 if r.g == 1 else 2))

        def workspace_free(eng, e):
            wait(eng, rows_folded, NG)
            wait(eng, projected, before(e, PROJ))
            wait(eng, mix_turned, before(e, (L1,)))

        block = ctx.enter_context(nc.Block())

        @block.sync
        def _(sp):
            for unit in range(UNITS):
                g, j, k, products, _ = LOADS[unit]
                source = a_cols if products == [L2T] else a_rows
                wait(sp, dve_unit, unit - RAW + 1)
                sp.dma_start(raw[:, unit % RAW, :], source[g * NU + j * VU + k])\
                    .then_inc(landed[unit % RAW], 16)
                if unit == RAW:
                    sp.dma_start(x[:, :, :], x_in.rearrange("(b p) f -> p b f", p=P)).then_inc(x_loaded, 16)
                    sp.dma_start(par[:, :], params).then_inc(params_in, 16)
                    for r in range(2):
                        sp.dma_start(brow[:, r, :], rows[r:r + 1, :].partition_broadcast(P)).then_inc(rows_in, 16)
                    sp.dma_start(alpha_col[:, :], alpha.partition_broadcast(P)).then_inc(rows_in, 16)
            for e in EPILOGUES:
                if e.p == L3:
                    sp.wait_ge(x_new, before(e, PROJ) + 1)
                    sp.dma_start(out.rearrange("(b p) f -> p b f", p=P)[:, e.g * GB:(e.g + 1) * GB, :],
                                 group(x, e.g)).then_inc(stored, 16)
            sp.wait_ge(stored, 16 * NG)

        @block.gpsimd
        def _(pool):
            nc.gpsimd.memset(ones[:, :], 1.0).then_inc(consts, 1)
            nc.gpsimd.memset(mhalf[:, :], -0.5).then_inc(consts, 1)
            nc.gpsimd.memset(ident[:, :], 0.0).then_inc(consts, 1)
            pool.wait_ge(consts, 3)
            nc.gpsimd.affine_select(out=ident[:, :], in_=ident[:, :], compare_op=ALU.not_equal, fill=1.0,
                                    base=0, pattern=[[-1, P]], channel_multiplier=1).then_inc(consts, 1)

            def reciprocal_std(k):
                pool.wait_ge(var_ready, k + 1)
                nc.gpsimd.tensor_tensor(rstd[:, :], veps[:, :], mhalf[:, :], ALU.pow).then_inc(rstd_ready, 1)

            for g in range(NG):
                reciprocal_std(g)
                pool.wait_ge(rows_saved, g + 1)
                nc.gpsimd.tensor_tensor(dgrp[:, :], dplus[:, :], mhalf[:, :], ALU.pow).then_inc(d_ready, 1)
            with pool.Fori(NG, len(NORM_OF)) as k:
                reciprocal_std(k)

        @block.scalar
        def _(act):
            act.wait_ge(consts, 4)
            nc.scalar.copy(ones_r[:, :], ones[:, :]).then_inc(rounded, 1)

            def normalize(k, g, half):
                act.wait_ge(shift_ready, shifts_before(k) + 1)
                wait(act, h_ready, k)
                for b in halves[half]:
                    last = nc.scalar.activation(tn[:, bass.ts(b, F)], x[:, g * GB + b, :], ACT.Relu,
                                                scale=rstd[:, b:b + 1], bias=shift[:, b:b + 1])
                if half == 1:
                    last.then_inc(normed, 1)

            def high_part(k, layer, g):
                act.wait_ge(normed, k + 1)
                nc.scalar.activation(group(h_high[layer % 2], g), blocks(tn), ACT.Relu).then_inc(high_ready, 1)

            def weight(g):
                act.wait_ge(normed, g + 1)
                act.wait_ge(d_ready, g + 1)
                for b in range(GB):
                    last = nc.scalar.activation(tn[:, bass.ts(b, F)], tn[:, bass.ts(b, F)], ACT.Relu,
                                                scale=dgrp[:, b:b + 1])
                last.then_inc(weighted, 1)
                act.wait_ge(weighted, g + 1)

            def take(r):
                act.wait_ge(pe_unit, splits_before(r.closed))
                if r.final and r.p != L1:
                    workspace_free(act, r.epilogue)
                    target = hsT if r.p == L2 else y
                else:
                    partial_free(act, r)
                    target = partial_of(r.p, r.g)[:, :]
                if r.p == L3:
                    nc.scalar.activation(target, acc[:, r.bank, :], ACT.Copy, scale=alpha_col[:, 0:1])\
                        .then_inc(act_take, 1)
                else:
                    nc.scalar.copy(target, acc[:, r.bank, :]).then_inc(act_take, 1)

            def take_self(e):
                act.wait_ge(self_turned, before(e, SELF) + 1)
                workspace_free(act, e)
                nc.scalar.copy(hsT, banks(2)).then_inc(selfT_ready, 1)

            def scale_projection(e):
                act.wait_ge(projected, before(e, PROJ) + 1)
                wait(act, x_new, before(e, PROJ))
                act.wait_ge(degrees_done, 2 if e.p == L2T else 1)
                for b in range(GB):
                    last = nc.scalar.activation(upd[:, bass.ts(b, F)], bank(b // CB)[:, bass.ts(b % CB, P)], ACT.Copy,
                                                scale=scale[e.p][:, e.g * GB + b:e.g * GB + b + 1])
                last.then_inc(scaled, 1)

            def message(e):
                act.wait_ge(msg_done, before(e, (L1,)) + 1)
                wait(act, projected, before(e, PROJ))
                nc.scalar.activation(msgT, banks(0), ACT.Relu, bias=cols[:, BMSG:BMSG + 1]).then_inc(msg_ready, 1)

            def gates(q):
                act.wait_ge(gates_done, q + 1)
                wait(act, mixed, q)
                nc.scalar.activation(gate_r, bank(2), ACT.Sigmoid, bias=gbias[:, 0:1]).then_inc(r_ready, 1)
                nc.scalar.activation(gate_z, bank(3), ACT.Sigmoid, bias=gbias[:, 1:2]).then_inc(z_ready, 1)

            def new_state(q):
                act.wait_ge(new_sum, q + 1)
                nc.scalar.activation(new_n, new_n, ACT.Tanh, bias=cols[:, BIH + 2:BIH + 3]).then_inc(n_ready, 1)

            def epilogue(e, at):
                if at == TAKE_AT and e.p == L1:
                    take_self(e)
                if e.p in ACT_SCALED and at == SCALE_AT[e.p]:
                    scale_projection(e)
                if e.p == L1:
                    if at == ACT_MSG_AT:
                        message(e)
                    for c in range(CH):
                        q = CH * before(e, (L1,)) + c
                        if at == ACT_GATES_AT[c]:
                            gates(q)
                        if at == ACT_NEW_AT[c]:
                            new_state(q)
                if e.p in ACT_NORMED:
                    for half in range(2):
                        if at == ACT_NORM_AT[e.p][half]:
                            normalize(NG + before(e, NORM), e.g, half)
                if e.p in NORM and at == HIGH_AT[e.p]:
                    high_part(NG + before(e, NORM), LAYER[e.p] + 1, e.g)

            for unit in range(UNITS + TAIL):
                for e in EPILOGUES:
                    epilogue(e, unit - e.start)
                for r in ACT_TAKES:
                    if take_unit(r) == unit:
                        take(r)
                for g in range(NG):
                    if unit == ROW_END[g] + ROW_HIGH_AT[g]:
                        weight(g)
                        high_part(g, 0, g)
                if unit not in SPLIT_NO:
                    continue
                _, j, k, _, sums = LOADS[unit]
                s = SPLIT_NO[unit]
                act.wait_ge(landed[unit % RAW], 16 * (unit // RAW + 1))
                wait(act, pe_unit, s - SPLIT + 1)
                if sums == "cols":
                    for jb in range(JB):
                        b = j * GB + k * JB + jb
                        last = nc.scalar.activation(a_high[:, s % SPLIT, bass.ts(jb, GC)],
                                                    raw[:, unit % RAW, bass.ts(jb, GC)], ACT.Copy,
                                                    accum_out=cpart[:, LOADS[unit][0], b:b + 1])
                    last.then_inc(act_unit, 1)
                else:
                    nc.scalar.copy(a_high[:, s % SPLIT, :], raw[:, unit % RAW, :]).then_inc(act_unit, 1)

        @block.vector
        def _(dve):
            done = [0]

            def step(ins):
                done[0] += 1
                ins.then_inc(small, 1)
                dve.wait_ge(small, done[0])

            def statistics(k, g, half):
                wait(dve, h_ready, k)
                for b in halves[half]:
                    last = nc.vector.bn_stats(stats[:, b, :], x[:, g * GB + b, :])
                if half == 0:
                    return
                last.then_inc(stats_done, 1)
                dve.wait_ge(stats_done, k + 1)
                for b in range(GB):
                    last = nc.vector.bn_aggr(mv[:, b, :], stats[:, b, :])
                last.then_inc(moments, 1)
                dve.wait_ge(moments, k + 1)
                nc.vector.tensor_scalar(veps[:, :], mv[:, :, 1], EPS, None, ALU.add).then_inc(var_ready, 1)

            def normalize(k, g):
                dve.wait_ge(rstd_ready, k + 1)
                for b in range(GB):
                    last = nc.vector.tensor_scalar(tn[:, bass.ts(b, F)], x[:, g * GB + b, :], mv[:, b, 0:1],
                                                   rstd[:, b:b + 1], ALU.subtract, ALU.mult)
                last.then_inc(normed, 1)

            def mean_shift(k):
                dve.wait_ge(rstd_ready, k + 1)
                nc.vector.scalar_tensor_tensor(out=shift[:, :], in0=mv[:, :, 0], scalar=-1.0, in1=rstd[:, :],
                                               op0=ALU.mult, op1=ALU.mult).then_inc(shift_ready, 1)

            def low_part(k, layer, g):
                dve.wait_ge(high_ready, k + 1)
                nc.vector.scalar_tensor_tensor(out=group(h_low[layer % 2], g), in0=blocks(tn), scalar=0.0,
                                               in1=group(h_high[layer % 2], g).bitcast(F32),
                                               op0=ALU.max, op1=ALU.subtract).then_inc(h_ready, 1)

            def own(e):
                layer = LAYER[e.p] % 2
                dve.wait_ge(h_ready, NORM_OF[LAYER[e.p], e.g] + 1)
                wait(dve, self_turned, before(e, SELF))
                wait(dve, mixed, CH * before(e, (L1,)))
                if e.p == L3:
                    wait(dve, projected, before(e, (L0, L2, L2T)))
                nc.vector.tensor_tensor(blocks(hsT if e.p == L3 else upd), group(h_high[layer], e.g).bitcast(F32),
                                        group(h_low[layer], e.g).bitcast(F32), ALU.add).then_inc(own_ready, 1)

            def add_own(e):
                dve.wait_ge(self_turned, before(e, SELF) + 1)
                if e.run.has_partial:
                    dve.wait_ge(act_take, ACT_TAKES[first_run(e.p, e.g)] + 1)
                    target = partial_of(e.p, e.g)[:, :]
                else:
                    sum_taken(dve, e.run)
                    target = y
                if e.p == L3:
                    ins = nc.vector.scalar_tensor_tensor(out=target, in0=banks(2), scalar=one_m_a[:, 0:1], in1=target,
                                                         op0=ALU.mult, op1=ALU.add)
                else:
                    ins = nc.vector.tensor_tensor(target, target, banks(2), ALU.add)
                ins.then_inc(self_added, 1)

            def take(r):
                dve.wait_ge(pe_unit, splits_before(r.closed))
                if r.p == L1:
                    target = partial[r.g][:, :]
                else:
                    workspace_free(dve, r.epilogue)
                    target = hsT if r.p == L2 else y
                dve.wait_ge(act_take, ACT_TAKES[first_run(r.p, r.g)] + 1)
                if r.p in (L0, L3):
                    dve.wait_ge(self_added, before(r.epilogue, (L0, L3)) + 1)
                if r.p == L3:
                    nc.vector.scalar_tensor_tensor(out=target, in0=acc[:, r.bank, :], scalar=alpha_col[:, 0:1],
                                                   in1=partial_of(r.p, r.g)[:, :], op0=ALU.mult, op1=ALU.add)\
                        .then_inc(dve_take, 1)
                else:
                    nc.vector.tensor_tensor(target, acc[:, r.bank, :], partial_of(r.p, r.g)[:, :], ALU.add)\
                        .then_inc(dve_take, 1)

            def degrees():
                dve.wait_ge(rows_in, 48)
                dve.wait_ge(params_in, 16)
                a = alpha_col[:, 0:1]
                step(nc.vector.tensor_tensor(gbias[:, :], cols[:, BIH:BIH + 2], cols[:, BHH:BHH + 2], ALU.add))
                step(nc.vector.tensor_scalar(one_m_a[:, :], a, -1.0, 1.0, ALU.mult, ALU.add))
                deg, sc = scale[L3], scale[L3]
                step(nc.vector.tensor_scalar(deg[:, :], rsum[:, :], a, one_m_a[:, 0:1], ALU.mult, ALU.add))
                step(nc.vector.tensor_scalar(flag[:, 1, :], deg[:, :], 0.0, None, ALU.is_equal))
                step(nc.vector.tensor_tensor(flag[:, 0, :], deg[:, :], flag[:, 1, :], ALU.add))
                step(nc.vector.reciprocal(deg[:, :], flag[:, 0, :]))
                step(nc.vector.tensor_scalar(flag[:, 1, :], flag[:, 1, :], -1.0, 1.0, ALU.mult, ALU.add))
                step(nc.vector.tensor_tensor(sc[:, :], deg[:, :], flag[:, 1, :], ALU.mult))
                guarded_reciprocal(rsum, scale[L2])

            def guarded_reciprocal(deg, sc):
                step(nc.vector.tensor_scalar(flag[:, 0, :], deg[:, :], 0.0, None, ALU.is_gt))
                step(nc.vector.tensor_scalar(flag[:, 1, :], flag[:, 0, :], -1.0, 1.0, ALU.mult, ALU.add))
                step(nc.vector.tensor_tensor(flag[:, 0, :], flag[:, 0, :], deg[:, :], ALU.mult))
                step(nc.vector.tensor_tensor(flag[:, 0, :], flag[:, 0, :], flag[:, 1, :], ALU.add))
                nc.vector.reciprocal(sc[:, :], flag[:, 0, :]).then_inc(degrees_done, 1)

            def column_degrees():
                dve.wait_ge(act_unit, splits_before(COLUMNS_DONE))
                dve.wait_ge(degrees_done, 1)
                step(nc.vector.tensor_reduce(csum[:, :], cpart[:, :, :].rearrange("p g b -> p b g"), AX.X, ALU.add))
                guarded_reciprocal(csum, scale[L2T])

            def sweep_steps(g, at):
                if at == ROW_STATS_AT:
                    if g == 0:
                        dve.wait_ge(x_loaded, 16)
                    statistics(g, g, 0)
                    statistics(g, g, 1)
                if at == ROW_NORM_AT:
                    normalize(g, g)
                if at == ROW_COPY_AT[g]:
                    dve.wait_ge(rows_folded, g + 1)
                    if REST_END[g] < ROW_END[g]:
                        dve.wait_ge(row_done, 1)
                    nc.vector.tensor_copy(rrow, E[0:1, row_bank(g):row_bank(g) + 2, :]
                                          .rearrange("p a b -> p (a b)")).then_inc(row_copied, 1)
                if at == ROW_SAVE_AT[g]:
                    dve.wait_ge(row_spread, g + 1)
                    sums = bank(row_bank(g))[:, 0:GB]
                    nc.vector.tensor_copy(rsum[:, bass.ts(g, GB)], sums)
                    nc.vector.tensor_scalar(dplus[:, :], sums, 1.0, None, ALU.add).then_inc(rows_saved, 1)
                if at == ROW_LOW_AT[g]:
                    low_part(g, 0, g)
                    nc.vector.tensor_copy(scale[L0][:, bass.ts(g, GB)], dgrp[:, :])

            def add_bias(g):
                dve.wait_ge(rows_in, 48)
                nc.vector.tensor_tensor(group(x, g), group(x, g),
                                        brow[:, BR0, :].unsqueeze(1).to_broadcast([P, GB, F]), ALU.add)\
                    .then_inc(bias_added, 1)

            def residual(e):
                v = before(e, PROJ)
                xg = group(x, e.g)
                if e.p in ACT_SCALED:
                    dve.wait_ge(scaled, before(e, ACT_SCALED) + 1)
                else:
                    dve.wait_ge(projected, v + 1)
                if e.p == L0:
                    dve.wait_ge(bias_added, sum(at <= BIAS_AT[e.g] for at in BIAS_AT))
                    for b in range(GB):
                        last = nc.vector.scalar_tensor_tensor(
                            out=xg[:, b, :], in0=bank(b // CB)[:, bass.ts(b % CB, P)],
                            scalar=scale[L0][:, e.g * GB + b:e.g * GB + b + 1], in1=xg[:, b, :],
                            op0=ALU.mult, op1=ALU.add)
                elif e.p == L3:
                    nc.vector.tensor_tensor(blocks(upd), blocks(upd),
                                            brow[:, BR3, :].unsqueeze(1).to_broadcast([P, GB, F]), ALU.add)\
                        .then_inc(biased, 1)
                    dve.wait_ge(biased, before(e, (L3,)) + 1)
                    last = nc.vector.scalar_tensor_tensor(out=xg, in0=blocks(upd), scalar=0.0, in1=xg,
                                                          op0=ALU.max, op1=ALU.add)
                else:
                    last = nc.vector.tensor_tensor(xg, xg, blocks(upd), ALU.add)
                last.then_inc(x_new, 1)
                dve.wait_ge(x_new, v + 1)

            def new_state(q):
                dve.wait_ge(r_ready, q + 1)
                nc.vector.scalar_tensor_tensor(out=new_n, in0=bank(0), scalar=cols[:, BHH + 2:BHH + 3], in1=gate_r,
                                               op0=ALU.add, op1=ALU.mult).then_inc(reset_done, 1)
                dve.wait_ge(reset_done, q + 1)
                nc.vector.tensor_tensor(new_n, new_n, bank(1), ALU.add).then_inc(new_sum, 1)

            def mix(q, c):
                dve.wait_ge(n_ready, q + 1)
                nc.vector.tensor_tensor(gate_r, hsT[:, bass.ts(c, BANK)], new_n, ALU.subtract).then_inc(mixing, 1)
                dve.wait_ge(mixing, 2 * q + 1)
                nc.vector.tensor_tensor(gate_r, gate_r, gate_z, ALU.mult).then_inc(mixing, 1)
                dve.wait_ge(mixing, 2 * q + 2)
                nc.vector.tensor_tensor(hsT[:, bass.ts(c, BANK)], gate_r, new_n, ALU.add).then_inc(mixed, 1)

            def gru_residual(e):
                dve.wait_ge(mix_turned, before(e, (L1,)) + 1)
                nc.vector.tensor_tensor(group(x, e.g), group(x, e.g), blocks(banks(2)), ALU.add).then_inc(x_gru, 1)

            def epilogue(e, at):
                if e.p in SELF and at == OWN_AT[e.p]:
                    own(e)
                if e.p in (L0, L3) and at == ADD_OWN_AT[e.run.has_partial]:
                    add_own(e)
                if e.p in PROJ and at == RESIDUAL_AT[e.p]:
                    residual(e)
                if e.p == L1:
                    for c in range(CH):
                        q = CH * before(e, (L1,)) + c
                        if at == DVE_NEW_AT[c]:
                            new_state(q)
                        if at == DVE_MIX_AT[c]:
                            mix(q, c)
                    if at == RESIDUAL_AT[L1]:
                        gru_residual(e)
                if e.p in NORM:
                    k = NG + before(e, NORM)
                    for half in range(2):
                        if at == STATS_AT[e.p][half]:
                            if e.p == L1:
                                dve.wait_ge(x_gru, before(e, (L1,)) + 1)
                            statistics(k, e.g, half)
                    if at == NORM_AT[e.p]:
                        if e.p in ACT_NORMED:
                            mean_shift(k)
                        else:
                            normalize(k, e.g)
                    if at == LOW_AT[e.p]:
                        low_part(k, LAYER[e.p] + 1, e.g)

            for unit in range(UNITS + TAIL):
                for e in EPILOGUES:
                    epilogue(e, unit - e.start)
                for r in DVE_TAKES:
                    if take_unit(r) == unit:
                        take(r)
                for g in range(NG):
                    sweep_steps(g, unit - ROW_END[g])
                    if unit == BIAS_AT[g]:
                        add_bias(g)
                if unit == SWEEP + 22:
                    degrees()
                if unit == COLUMNS_DONE + SPLIT:
                    column_degrees()
                if unit >= UNITS:
                    continue
                products = LOADS[unit][3]
                new = raw[:, unit % RAW, :]
                dve.wait_ge(landed[unit % RAW], 16 * (unit // RAW + 1))
                if products:
                    s = SPLIT_NO[unit]
                    dve.wait_ge(act_unit, s + 1)
                    wait(dve, pe_unit, s - SPLIT + 1)
                    nc.vector.tensor_tensor(a_low[:, s % SPLIT, :], new, a_high[:, s % SPLIT, :].bitcast(F32),
                                            ALU.subtract).then_inc(dve_unit, 1)
                elif unit == REST[LOADS[unit][0]][0]:
                    wait(dve, rows_folded, LOADS[unit][0])
                    nc.vector.tensor_copy(ybuf[:, :], new).then_inc(dve_unit, 1)
                else:
                    dve.wait_ge(dve_unit, unit)
                    nc.vector.tensor_tensor(ybuf[:, :], ybuf[:, :], new, ALU.add).then_inc(dve_unit, 1)

        @block.tensor
        def _(pe):
            pe.wait_ge(consts, 4)
            pe.wait_ge(rounded, 1)

            def fold_rows(g):
                pe.wait_ge(dve_unit, REST_END[g])
                wait(pe, rows_saved, g - 1)
                alone = shared_before(g, REST_END[g]) == 0
                for c in range(CH):
                    for jb in range(JB):
                        last = nc.tensor.matmul(bank(row_bank(g) + c), ones[:, :], ybuf[:, jb * GC + c * BANK:jb * GC + (c + 1) * BANK],
                                                start=alone and jb == 0,
                                                stop=REST_END[g] == ROW_END[g] and jb == JB - 1)
                last.then_inc(rows_folded, 1)

            def spread_rows(g):
                pe.wait_ge(row_copied, g + 1)
                for b in range(GB):
                    last = nc.tensor.matmul(bank(row_bank(g))[:, b:b + 1], rrow[:, bass.ts(b, P)], ones[0:1, 0:1],
                                            start=True, stop=True)
                last.then_inc(row_spread, 1)

            def turn_self(e):
                pe.wait_ge(rows_saved, NG)
                pe.wait_ge(own_ready, before(e, SELF) + 1)
                wait(pe, selfT_ready, before(e, (L1,)))
                wait(pe, self_added, before(e, (L0, L3)))
                wait(pe, z_ready, CH * before(e, (L1,)))
                wait(pe, x_gru, before(e, (L1,)))
                source = hsT if e.p == L3 else upd
                for b in range(GB):
                    last = nc.tensor.transpose(bank(2 + b // CB)[:, bass.ts(b % CB, P)], source[:, bass.ts(b, P)],
                                               ident[:, :])
                last.then_inc(self_turned, 1)

            def project(e):
                sum_taken(pe, e.run)
                wait(pe, x_new, before(e, PROJ))
                wait(pe, new_sum, CH * before(e, (L1,)))
                pe.wait_ge(rows_saved, NG)
                if e.p in (L0, L3):
                    pe.wait_ge(self_added, before(e, (L0, L3)) + 1)
                source = hsT if e.p == L2 else y
                for b in range(GB):
                    last = nc.tensor.matmul(bank(b // CB)[:, bass.ts(b % CB, P)], source[:, bass.ts(b, P)],
                                            w(WEIGHT[e.p]), start=True, stop=True)
                last.then_inc(projected, 1)

            def message(e):
                sum_taken(pe, e.run)
                pe.wait_ge(x_new, before(e, PROJ))
                wait(pe, new_sum, CH * before(e, (L1,)))
                for c in range(CH):
                    last = nc.tensor.matmul(bank(c), w(WMSG), partial[e.g][:, bass.ts(c, BANK)], start=True, stop=True)
                last.then_inc(msg_done, 1)

            def gates(e, q, c):
                m, h = msgT[:, bass.ts(c, BANK)], hsT[:, bass.ts(c, BANK)]
                pe.wait_ge(selfT_ready, before(e, (L1,)) + 1)
                if c > 0:
                    pe.wait_ge(z_ready, q)
                for i in range(2):
                    nc.tensor.matmul(bank(2 + i), w(WHH + i), h, start=True, stop=False)
                pe.wait_ge(msg_ready, before(e, (L1,)) + 1)
                for i in range(2):
                    nc.tensor.matmul(bank(2 + i), w(WIH + i), m, start=False, stop=True)
                if c > 0:
                    pe.wait_ge(new_sum, q)
                nc.tensor.matmul(bank(0), w(WHH + 2), h, start=True, stop=True)
                nc.tensor.matmul(bank(1), w(WIH + 2), m, start=True, stop=True).then_inc(gates_done, 1)

            def turn_mix(e):
                pe.wait_ge(mixed, CH * (before(e, (L1,)) + 1))
                for b in range(GB):
                    last = nc.tensor.transpose(bank(2 + b // CB)[:, bass.ts(b % CB, P)], hsT[:, bass.ts(b, P)],
                                               ident[:, :])
                last.then_inc(mix_turned, 1)

            def epilogue(e, at):
                if e.p in SELF and at == TURN_AT[e.p]:
                    turn_self(e)
                if e.p in PROJ and at == PROJECT_AT[e.p]:
                    project(e)
                if e.p == L1:
                    if at == MSG_AT:
                        message(e)
                    for c in range(CH):
                        if at == GATES_AT[c]:
                            gates(e, CH * before(e, (L1,)) + c, c)
                    if at == MIX_AT:
                        turn_mix(e)

            def multiply(unit):
                g, j, k, products, sums = LOADS[unit]
                s = SPLIT_NO[unit]
                slot = s % SPLIT
                mine = [r for r in RUNS if r.p in products and r.g == g and r.first <= unit <= r.last]
                pe.wait_ge(act_unit, s + 1)

                def column(jb, c):
                    return slice(jb * GC + c * BANK, jb * GC + (c + 1) * BANK)

                for r in mine:
                    if k == 0:
                        pe.wait_ge(h_ready, NORM_OF[LAYER[r.p], j] + 1)
                    if unit == r.first and r.before is not None:
                        sum_taken(pe, r.before)
                    high, low = h_high[LAYER[r.p] % 2], h_low[LAYER[r.p] % 2]
                    for jb in range(JB):
                        b = j * GB + k * JB + jb
                        for part in (high, low):
                            for c in range(CH):
                                nc.tensor.matmul(acc[:, r.bank, bass.ts(c, BANK)], part[:, b, :],
                                                 a_high[:, slot, column(jb, c)],
                                                 start=unit == r.first and jb == 0 and part is high,
                                                 stop=False)
                last_of_row = sums == "rows" and unit == ROW_END[g] - 1
                if sums == "rows":
                    first_of_row = shared_before(g, unit) == 0
                    if first_of_row:
                        wait(pe, rows_saved, g - 1)
                    for jb in range(JB):
                        for c in range(CH):
                            nc.tensor.matmul(bank(row_bank(g) + c), ones_r[:, :], a_high[:, slot, column(jb, c)],
                                             start=first_of_row and jb == 0, stop=False)
                pe.wait_ge(dve_unit, unit + 1)
                if sums == "rows":
                    for jb in range(JB):
                        for c in range(CH):
                            last = nc.tensor.matmul(bank(row_bank(g) + c), ones_r[:, :], a_low[:, slot, column(jb, c)],
                                                    start=False, stop=last_of_row and jb == JB - 1)
                    if last_of_row:
                        last.then_inc(row_done, 1)
                for r in mine:
                    for jb in range(JB):
                        b = j * GB + k * JB + jb
                        for c in range(CH):
                            last = nc.tensor.matmul(acc[:, r.bank, bass.ts(c, BANK)],
                                                    h_high[LAYER[r.p] % 2][:, b, :], a_low[:, slot, column(jb, c)],
                                                    start=False, stop=unit == r.last and jb == JB - 1)
                last.then_inc(pe_unit, 1)

            for unit in range(UNITS + TAIL):
                for g in range(NG):
                    if unit == REST_END[g]:
                        fold_rows(g)
                    if unit == ROW_END[g] + ROW_SPREAD_AT[g]:
                        spread_rows(g)
                if unit == SWEEP:
                    pe.wait_ge(params_in, 16)
                for e in EPILOGUES:
                    epilogue(e, unit - e.start)
                if unit in SPLIT_NO:
                    multiply(unit)


def kernel(**inputs):
    import numpy as np
    import concourse.bacc as bacc
    from concourse.bass_utils import run_bass_kernel_spmd

    def tiles(a):
        return np.ascontiguousarray(
            a.reshape(NU, JB, P, NG, GC).transpose(3, 0, 2, 1, 4).reshape(NG * NU, P, JB * GC))

    a = {k: np.asarray(v) for k, v in inputs.items()}
    params = np.concatenate([
        a["L0_gnn_W"].T, a["L1_gnn_W_msg"].T, a["L1_gnn_W_ih"].T, a["L1_gnn_W_hh"].T, a["L2_gnn_W_in"],
        a["L2_gnn_W_out"], a["L3_gnn_W"].T, a["L1_gnn_b_msg"][:, None], a["L1_gnn_b_ih"].reshape(3, F).T,
        a["L1_gnn_b_hh"].reshape(3, F).T], axis=1)
    arrays = {
        "x_in": np.ascontiguousarray(a["x"]), "a_rows": tiles(a["adj"].T), "a_cols": tiles(a["adj"]),
        "params": np.ascontiguousarray(params), "rows": np.stack([a["L0_gnn_b"], a["L3_gnn_b"]]),
        "alpha": a["L3_gnn_alpha"].reshape(1, 1),
    }
    nc = bacc.Bacc("TRN2", target_bir_lowering=False, num_devices=1)
    f32 = mybir.dt.float32
    aps = {k: nc.dram_tensor(k, v.shape, f32, kind="ExternalInput").ap() for k, v in arrays.items()}
    out = nc.dram_tensor("out", (N, F), f32, kind="ExternalOutput").ap()
    build_gnn(nc, out=out, **aps)
    r = run_bass_kernel_spmd(nc, [arrays], core_ids=[0])
    return r.results[0]["out"]
```
